# Optimizing a Trainium2 kernel written in Bass

```python
import numpy as np
import jax
import jax.numpy as jnp

def _softmax(x, axis=-1):
    return jax.nn.softmax(x, axis=axis)

def _gelu(x):
    return jax.nn.gelu(x, approximate=True)

def _silu(x):
    return jax.nn.silu(x)

def _sigmoid(x):
    return jax.nn.sigmoid(x)

def _layernorm(x, axis=-1, eps=1e-05):
    m = jnp.mean(x, axis=axis, keepdims=True)
    v = jnp.var(x, axis=axis, keepdims=True)
    return (x - m) / jnp.sqrt(v + eps)

def _scatter_add(tgt, idx, src, axis=0):
    return tgt.at[idx].add(src)

def _segment_sum(src, seg, n):
    return jax.ops.segment_sum(src, seg, n)
kernel_name = 'mk_flamingo_gated_d1_seqx_r4_0f2245'

def setup_inputs(seed: int=0):
    np.random.seed(seed)
    _w = jnp.asarray

    def _rec_inputs():
        import jax
        import jax.numpy as jnp
        _rk = jax.random.key(seed)
        x = -0.0003929 + 0.9999 * jax.random.normal(jax.random.fold_in(_rk, 1), (8, 512, 256), jnp.float32)
        _lenS = 512 - jax.random.randint(jax.random.fold_in(_rk, 7), (8,), 0, max(1, 512 // 4) + 1, jnp.int32)
        _lenS2 = 1024 - jax.random.randint(jax.random.fold_in(_rk, 8), (8,), 0, max(1, 1024 // 4) + 1, jnp.int32)
        _ctx_2048P = jax.random.normal(jax.random.fold_in(_rk, 11), (8, 16, 512), jnp.float32)
        _ctx_2048c = jax.random.dirichlet(jax.random.fold_in(_rk, 511), 0.3 * jnp.ones((16,), jnp.float32), (8, 1024))
        _ctx_2048t = jnp.einsum('bsk,bkd->bsd', _ctx_2048c, _ctx_2048P)
        _ctx_2048t = _ctx_2048t * jax.lax.rsqrt(jnp.mean(jnp.square(_ctx_2048t)) + 1e-12) * 0.953939
        ctx_2048 = 4.13588e-05 + 0.999923 * (_ctx_2048t + 0.3 * jax.random.normal(jax.random.fold_in(_rk, 611), (8, 1024, 512), jnp.float32))
        _validS = jnp.arange(512)[None, :] < _lenS[:, None]
        _validS2 = jnp.arange(1024)[None, :] < _lenS2[:, None]
        _causal = jnp.tril(jnp.ones((512, 512), dtype=bool))
        mask_BxS2_if0 = jnp.where(jnp.ones((8, 1024), dtype=bool), 4, 0).astype(jnp.int32)
        _g = jax.random.normal(jax.random.fold_in(_rk, 9001), (2, 1), jnp.float32)
        _g = jnp.sign(_g) * jnp.maximum(jnp.abs(_g), 1.0) + (_g == 0) * 1.0
        g_xattn = _g[0]
        g_ffn = _g[1]
        return (x, ctx_2048, mask_BxS2_if0, g_xattn, g_ffn)
    x, ctx_2048, mask_BxS2_if0, g_xattn, g_ffn = _rec_inputs()

    def _L0_xattn_setup():
        import jax, jax.numpy as jnp
        import numpy as np
        B, L, P = (4, 1024, 256)
        D_MODEL = 256
        D_GLOBAL = 512
        HEADDIM = 32
        EPSILON = 0.001
        RMS_EPS = 1e-05

        def rmsnorm(x, g, eps=RMS_EPS):
            var = jnp.mean(jnp.square(x), axis=-1, keepdims=True)
            return x * jax.lax.rsqrt(var + eps) * g

        def _hnet_depool(h, h_patch_full, patch_lens):
            h_patch = h_patch_full[..., :D_MODEL]
            bsz, plen = (h_patch.shape[0], h_patch.shape[1])
            seqlen = h.shape[1]
            logp = jnp.full((bsz, plen), -EPSILON, dtype=jnp.float32)
            bidx = jnp.cumsum(patch_lens, axis=1) - 1
            boundary_mask = jnp.zeros((bsz, seqlen), dtype=jnp.int32)
            boundary_mask = boundary_mask.at[jnp.arange(bsz)[:, None], bidx].set(1)
            dt = (-jnp.log(-jnp.expm1(logp))).astype(h_patch.dtype)
            x = h_patch / dt[..., None]
            n_heads = D_MODEL // HEADDIM
            A = -jnp.ones((n_heads,), dtype=jnp.float32)
            bcoef = jnp.exp(logp).astype(h_patch.dtype)
            x4 = x.reshape(bsz, plen, n_heads, HEADDIM)
            a = jnp.exp(dt[:, :, None] * A[None, None, :])
            u = (dt * bcoef)[:, :, None, None] * x4
            a_b = jnp.broadcast_to(a[..., None], u.shape)

            def comb(lft, rgt):
                aL, uL = lft
                aR, uR = rgt
                return (aL * aR, uL * aR + uR)
            _, s = jax.lax.associative_scan(comb, (a_b, u), axis=1)
            depool = s.reshape(bsz, plen, D_MODEL)
            plug = jnp.clip(jnp.cumsum(boundary_mask, axis=1) - 1, 0, plen - 1)
            depool_out = depool[jnp.arange(bsz)[:, None], plug]
            return depool_out + h
        key = jax.random.key(seed)
        k1, k2, k3, k4 = jax.random.split(key, 4)
        embeds = jax.random.normal(k1, (B, L, D_MODEL), dtype=jnp.float32)
        patch_embeds = jax.random.normal(k2, (B, P, D_GLOBAL), dtype=jnp.float32)
        patch_lens = jnp.full((B, P), L // P, dtype=jnp.int64)
        W_in = jax.random.normal(k3, (D_MODEL, D_MODEL), dtype=jnp.float32) * 0.02
        b_in = jnp.zeros((D_MODEL,), dtype=jnp.float32)
        g_res = jnp.ones((D_MODEL,), dtype=jnp.float32)
        g_init = jnp.ones((D_GLOBAL,), dtype=jnp.float32)
        return {'embeds': embeds, 'patch_embeds': patch_embeds, 'patch_lens': patch_lens, 'W_in': W_in, 'b_in': b_in, 'g_res': g_res, 'g_init': g_init}
    _L0_xattn_all = _L0_xattn_setup()
    _L0_xattn_in = {k: v for k, v in _L0_xattn_all.items() if k in ('W_in', 'b_in', 'g_res', 'g_init')}
    del _L0_xattn_all

    def _L0_ffn_setup():
        import jax, jax.numpy as jnp
        import numpy as np
        key = jax.random.key(seed)
        k1, k2, k3, k4, k5 = jax.random.split(key, 5)
        d_in, d_out, r = (256, 256, 32)
        x = jax.random.normal(k1, (8, 2048, d_in), dtype=jnp.float32)
        W = jax.random.normal(k2, (d_out, d_in), dtype=jnp.float32) * (1.0 / np.sqrt(d_in))
        b = jax.random.normal(k3, (d_out,), dtype=jnp.float32) * 0.01
        V_r = jax.random.normal(k4, (d_in, r), dtype=jnp.float32) * (1.0 / np.sqrt(d_in))
        C = jax.random.normal(k5, (d_out, r), dtype=jnp.float32) * (1.0 / np.sqrt(r))
        return {'x': x, 'W': W, 'b': b, 'V_r': V_r, 'C': C}
    _L0_ffn_all = _L0_ffn_setup()
    _L0_ffn_in = {k: v for k, v in _L0_ffn_all.items() if k in ('W', 'b', 'V_r', 'C')}
    del _L0_ffn_all
    return {'x': x, 'ctx_2048': ctx_2048, 'mask_BxS2_if0': mask_BxS2_if0, 'g_xattn': g_xattn, 'g_ffn': g_ffn, 'L0_xattn_W_in': _L0_xattn_in['W_in'], 'L0_xattn_b_in': _L0_xattn_in['b_in'], 'L0_xattn_g_res': _L0_xattn_in['g_res'], 'L0_xattn_g_init': _L0_xattn_in['g_init'], 'L0_ffn_W': _L0_ffn_in['W'], 'L0_ffn_b': _L0_ffn_in['b'], 'L0_ffn_V_r': _L0_ffn_in['V_r'], 'L0_ffn_C': _L0_ffn_in['C']}

def reference(x, ctx_2048, mask_BxS2_if0, g_xattn, g_ffn, L0_xattn_W_in, L0_xattn_b_in, L0_xattn_g_res, L0_xattn_g_init, L0_ffn_W, L0_ffn_b, L0_ffn_V_r, L0_ffn_C):
    import jax
    import jax.numpy as jnp

    def _L0_xattn_ref(embeds, patch_embeds, patch_lens, W_in, b_in, g_res, g_init):
        import jax, jax.numpy as jnp
        import numpy as np
        B, L, P = (4, 1024, 256)
        D_MODEL = 256
        D_GLOBAL = 512
        HEADDIM = 32
        EPSILON = 0.001
        RMS_EPS = 1e-05

        def rmsnorm(x, g, eps=RMS_EPS):
            var = jnp.mean(jnp.square(x), axis=-1, keepdims=True)
            return x * jax.lax.rsqrt(var + eps) * g

        def _hnet_depool(h, h_patch_full, patch_lens):
            h_patch = h_patch_full[..., :D_MODEL]
            bsz, plen = (h_patch.shape[0], h_patch.shape[1])
            seqlen = h.shape[1]
            logp = jnp.full((bsz, plen), -EPSILON, dtype=jnp.float32)
            bidx = jnp.cumsum(patch_lens, axis=1) - 1
            boundary_mask = jnp.zeros((bsz, seqlen), dtype=jnp.int32)
            boundary_mask = boundary_mask.at[jnp.arange(bsz)[:, None], bidx].set(1)
            dt = (-jnp.log(-jnp.expm1(logp))).astype(h_patch.dtype)
            x = h_patch / dt[..., None]
            n_heads = D_MODEL // HEADDIM
            A = -jnp.ones((n_heads,), dtype=jnp.float32)
            bcoef = jnp.exp(logp).astype(h_patch.dtype)
            x4 = x.reshape(bsz, plen, n_heads, HEADDIM)
            a = jnp.exp(dt[:, :, None] * A[None, None, :])
            u = (dt * bcoef)[:, :, None, None] * x4
            a_b = jnp.broadcast_to(a[..., None], u.shape)

            def comb(lft, rgt):
                aL, uL = lft
                aR, uR = rgt
                return (aL * aR, uL * aR + uR)
            _, s = jax.lax.associative_scan(comb, (a_b, u), axis=1)
            depool = s.reshape(bsz, plen, D_MODEL)
            plug = jnp.clip(jnp.cumsum(boundary_mask, axis=1) - 1, 0, plen - 1)
            depool_out = depool[jnp.arange(bsz)[:, None], plug]
            return depool_out + h
        h = rmsnorm(embeds, g_res)
        h = jnp.einsum('bld,ed->ble', h, W_in) + b_in
        h_patch = rmsnorm(patch_embeds, g_init)
        return _hnet_depool(h, h_patch, patch_lens)

    def _L0_ffn_ref(x, W, b, V_r, C):
        import jax, jax.numpy as jnp
        import numpy as np
        base = jnp.einsum('bsd,od->bso', x, W) + b
        correction = jnp.einsum('bsr,or->bso', jnp.einsum('bsd,dr->bsr', x, V_r), C)
        return base + correction
    x = x + jnp.tanh(g_xattn[0]) * _L0_xattn_ref(_layernorm(x, axis=-1), ctx_2048, mask_BxS2_if0, L0_xattn_W_in, L0_xattn_b_in, L0_xattn_g_res, L0_xattn_g_init)
    x = x + jnp.tanh(g_ffn[0]) * _L0_ffn_ref(_layernorm(x, axis=-1), L0_ffn_W, L0_ffn_b, L0_ffn_V_r, L0_ffn_C)
    return x

_drawn_inputs = setup_inputs


def setup_inputs(seed=0):
    import zlib

    import numpy as np

    out = dict(_drawn_inputs(seed))
    spreads = {'L0_xattn_b_in': (0.0, 0.1), 'L0_xattn_g_res': (1.0, 0.2), 'L0_xattn_g_init': (1.0, 0.2)}
    factors = {'L0_ffn_b': 8.0}
    for name, (base, spread) in spreads.items():
        noise = np.random.default_rng([zlib.crc32(name.encode()), seed]).standard_normal(out[name].shape)
        drawn = base * np.exp(spread * noise) if base else spread * noise
        out[name] = jnp.asarray(drawn.astype(out[name].dtype))
    for name, factor in factors.items():
        out[name] = (out[name] * factor).astype(out[name].dtype)
    return out
```

```python
from contextlib import ExitStack

import concourse.bass as bass
import numpy as np
from concourse import mybir

F32 = mybir.dt.float32
F32R = mybir.dt.float32r
F16 = mybir.dt.float16
BF16 = mybir.dt.bfloat16
I32 = mybir.dt.int32
ALU = mybir.AluOpType
ACT = mybir.ActivationFunctionType

B, S, D = 8, 512, 256
NP, DG = 1024, 512
R = 32
P = 128
KB = D // P
TPB = S // P
NPAIR = 2 * B
QT = S // P
EPS = 1e-5
LO = 16
HI = S // LO
PT = NP // P
EPS_DT = 0.001
DT = -np.log(-np.expm1(-EPS_DT))
C_ID, C_DEC, C_CORN, C_LO, C_Q, C_END = 0, 128, 256, 384, 400, 404


def build_gated_depool_ffn(nc: bass.Bass, x, ctx, mask, g_x, g_f, w_in_t, b_in, g_res, g_init, w_t, b_f, v_t, c_t,
                           consts, masks, out):
    es = ExitStack()
    with es:
        def sb(name, shape, dt=F32):
            return es.enter_context(nc.sbuf_tensor(name, shape, dt))

        def ps(name, shape):
            return es.enter_context(nc.psum_tensor(name, shape, F32))

        def sem(name):
            return es.enter_context(nc.semaphore(name))

        con = sb("con", [P, C_END])
        msk = sb("msk", [P, 2 * P + B], F16)
        ident = con[:, C_ID:C_ID + P]
        decay_t = con[:, C_DEC:C_DEC + P]
        lo_eye = con[:, C_LO:C_LO + LO]
        q_index = con[:, C_Q:C_Q + 1]
        batch_prefix, batch_ones, batch_pick = msk[:, 0:P], msk[:, P:2 * P], msk[:, 2 * P:]
        neg_ident = sb("neg_ident", [P, P], F32R)
        mean_w = sb("mean_w", [P, P])
        gates = sb("gates", [P, 2])
        tg = sb("tg", [P, 2])
        gres_sb = sb("gres_sb", [P, KB])
        ginit_b = sb("ginit_b", [P, D])
        b1_b = sb("b1_b", [P, D])
        b2_b = sb("b2_b", [P, D])
        w1_raw = sb("w1_raw", [P, KB, D])
        w1_f = sb("w1_f", [P, KB, D])
        w1_hi = sb("w1_hi", [P, KB, D], F32R)
        w1_lo = sb("w1_lo", [P, KB, D], F32R)
        w2_raw = sb("w2_raw", [P, KB, D])
        w2_f = sb("w2_f", [P, KB, D])
        w2_hi = sb("w2_hi", [P, KB, D], F32R)
        w2_lo = sb("w2_lo", [P, KB, D], F32R)
        v_sb = sb("v_sb", [R, D])
        c_sb = sb("c_sb", [R, D])
        lens = sb("lens", [B, NP], I32)
        ones_s = sb("ones_s", [P, NP])
        ends = sb("ends", [B, NP])
        wrap = sb("wrap", [P, PT * B])
        bidx = sb("bidx", [P, PT * B])
        bidx_i = sb("bidx_i", [P, PT * B], I32)
        bhi_i = sb("bhi_i", [P, PT * B], I32)
        blo_i = sb("blo_i", [P, PT * B], I32)
        bhi = sb("bhi", [P, PT * B], BF16)
        blo = sb("blo", [P, PT * B], BF16)
        iota_hi = sb("iota_hi", [P, HI, PT * B], BF16)
        hot_hi = sb("hot_hi", [P, HI, PT * B], BF16)
        hot_lo = sb("hot_lo", [P, LO, PT * B], BF16)
        bound = sb("bound", [HI, B * LO])
        bound_t = sb("bound_t", [P, HI], F16)
        row_scan = sb("row_scan", [P, HI])
        row_ex = sb("row_ex", [P, HI])
        count = sb("count", [P, HI])
        plug = sb("plug", [P, HI])
        plug_x = sb("plug_x", [P, S], F16)
        beyond = sb("beyond", [P, 1])
        flag = sb("flag", [1, 1], I32)
        x_sb = sb("x_sb", [P, 2, 2, 2, D])
        xn_sb = sb("xn_sb", [P, 2, 2, D])
        x1_sb = sb("x1_sb", [P, 2, 2, 2, D])
        out_sb = sb("out_sb", [P, 2, 2, 2, D])
        xt_hi = sb("xt_hi", [P, 2, 4, P], F32R)
        xt_lo = sb("xt_lo", [P, 2, 4, P], F32R)
        x1t_hi = sb("x1t_hi", [P, 2, 4, P], F32R)
        x1t_lo = sb("x1t_lo", [P, 2, 4, P], F32R)
        bn1 = sb("bn1", [P, 2, 2, 2, 6])
        mv1 = sb("mv1", [P, 2, 2, 2, 2])
        std1 = sb("std1", [P, 2, 2, 2])
        s1 = sb("s1", [P, 2, 2, 2])
        m1 = sb("m1", [P, 2, 2, 2])
        bn2 = sb("bn2", [P, 2, 2, 2, 6])
        mv2 = sb("mv2", [P, 2, 2, 2, 2])
        std2 = sb("std2", [P, 2, 2, 2])
        s2 = sb("s2", [P, 2, 2, 2])
        ctx_sb = sb("ctx_sb", [P, 2, DG])
        ctx_sq = sb("ctx_sq", [P, DG])
        c_ss = sb("c_ss", [P, 2])
        c_std = sb("c_std", [P, 2])
        c_r = sb("c_r", [P, 2])
        u_sb = sb("u_sb", [P, D])
        dp_g = sb("dp_g", [P, D])
        dp_f = sb("dp_f", [P, D])
        dp_hi = sb("dp_hi", [P, 2, D], F32R)
        dp_lo = sb("dp_lo", [P, 2, D], F32R)
        pick = sb("pick", [P, 2, TPB, P], F32R)

        g_ctx = sb("g_ctx", [P, QT, DG])
        g_ss = sb("g_ss", [P, QT])
        g_std = sb("g_std", [P, QT])
        g_inv = sb("g_inv", [P, QT])
        g_u = sb("g_u", [P, QT, D])
        g_dp = sb("g_dp", [P, QT, D])
        g_pick = sb("g_pick", [P, QT, S])
        r_x = sb("r_x", [P, TPB, D])
        g_n = sb("g_n", [P, TPB, D])
        g_t = sb("g_t", [P, TPB, KB, P])
        g_x1 = sb("g_x1", [P, TPB, D])
        g_bn = sb("g_bn", [P, TPB, 6])
        g_mv = sb("g_mv", [P, TPB, 2])

        t1_ps = ps("t1_ps", [P, 4, P])
        t2_ps = ps("t2_ps", [P, 4, P])
        a_ps = [ps(f"a_ps{n}", [P, 2, D]) for n in range(2)]
        b_ps = [ps(f"b_ps{n}", [P, 2, D]) for n in range(2)]
        dp_ps = ps("dp_ps", [P, 2 * D])
        plug_ps = ps("plug_ps", [P, S])
        ends_ps = t1_ps[:].rearrange("p a b -> p (a b)")[:, 0:PT * B]
        count_ps = t2_ps[:].rearrange("p a b -> p (a b)")
        bound_ps = dp_ps[:, 0:HI]
        prefix_ps = plug_ps[:, 0:HI]
        total_ps = plug_ps[:, 256:256 + HI]
        corr_ps = b_ps[0]
        mean_ps = b_ps[1][:, 0, :]
        flag_ps = dp_ps[0:1, 256:257]

        x_v = x.rearrange("b (p h j) d -> b p h (j d)", p=P, h=2)
        out_v = out.rearrange("b (p h j) d -> b p h (j d)", p=P, h=2)

        names = ("lens_in", "w_in", "con_in", "g_in", "iotas", "consts_made", "v_done", "ends_t", "scanned",
                 "hots", "counted", "bound_r", "bound_tr", "bound_h", "prefixed", "rows_scanned", "rows_ex", "counts", "plugs", "plug_xed",
                 "flag_mm", "flag_set", "tanh_done", "w1_ready", "w1_hi_ready", "w2_corr", "w2_full", "w2_mean", "w2_cen", "w2_hi_ready",
                 "w_split", "b_scaled",
                 "t1_done", "hi1", "lo1_mm", "lo1", "a_done", "x1_done", "t2_done", "hi2", "lo2_mm", "lo2", "b_done",
                 "stats1", "std1_s", "s1_done", "xn_done", "stats2", "std2_s", "s2_done", "x1b_done", "out_done",
                 "ctx_sqd", "ctx_std", "ctx_r", "u_done", "dp_mm", "dpg_done", "dpf_done", "dph_done", "dpl_done",
                 "plug_mm", "pick_done", "aggr1", "aggr2", "idx_w", "idx_f", "idx_i", "carrier", "inv1")
        s = {n: sem(n) for n in names}
        x_in = [[sem(f"x_in{q}{h}") for h in range(2)] for q in range(2)]
        ctx_in = [sem(f"ctx_in{q}") for q in range(2)]
        out_free = [[sem(f"out_free{q}{h}") for h in range(2)] for q in range(2)]

        g = {n: sem("g_" + n) for n in (
            "stored", "ctx_in", "x_in", "squared", "ctx_std", "ctx_inv", "u", "scanned", "dp", "spread", "picks",
            "bn1", "mv1", "std1", "inv1", "xn", "t1", "t1_read", "mixed", "x1", "bn2", "mv2", "std2", "inv2",
            "t2", "t2_read", "product", "scaled", "out")}

        block = es.enter_context(nc.Block())

        def flagged(eng):
            eng.wait_ge(s["flag_set"], 1)
            return eng.value_load(flag[0:1, 0:1], min_val=0, max_val=P) > 0

        def wait(eng, name, value):
            if isinstance(value, int) and value <= 0:
                return
            eng.wait_ge(s[name], value)

        def wait_apart(eng, name, value):
            wait(eng, name, value)
            if not isinstance(value, int):
                eng.sem_inc(s["carrier"], 1)

        @block.sync
        def _(sp):
            sp.dma_start(lens[:], mask).then_inc(s["lens_in"], 16)

            def load_x(b, q, h):
                sp.dma_start(x_sb[:, q, h, :, :].rearrange("p j d -> p (j d)"), x_v[b, :, h, :]).then_inc(x_in[q][h], 16)

            def load_ctx(b, q):
                sp.dma_start(ctx_sb[:, q, :], ctx[b, 0:P, :]).then_inc(ctx_in[q], 16)

            for b in (0, 1):
                for h in (0, 1):
                    load_x(b, b, h)
                    if (b, h) == (0, 0):
                        sp.dma_start(con[:], consts).then_inc(s["con_in"], 16)
                        sp.dma_start(msk[:], masks).then_inc(s["con_in"], 16)
                load_ctx(b, b)

            def step(b, q, load, store):
                i = 2 * b
                for h in (0, 1):
                    if load:
                        wait(sp, "x1_done", i + h + 1)
                        load_x(b + 2, q, h)
                        if h == 0:
                            wait(sp, "u_done", b + 1)
                            load_ctx(b + 2, q)
                    if store:
                        wait(sp, "out_done", i + h - 1)
                        sp.dma_start(out_v[b - 1, :, h, :], out_sb[:, 1 - q, h, :, :].rearrange("p j d -> p (j d)")
                                     ).then_inc(out_free[1 - q][h], 16)

            step(0, 0, True, False)
            with sp.Fori(0, 2) as k:
                step(2 * k + 1, 1, True, True)
                step(2 * k + 2, 0, True, True)
            step(5, 1, True, True)
            for b in (6, 7, 8):
                step(b, b % 2, False, True)
            for q in (0, 1):
                for h in (0, 1):
                    sp.wait_ge(out_free[q][h], 16 * (B // 2 + 1))
            with sp.If(flagged(sp)):
                sp.sem_inc(g["stored"], 16)
                with sp.Fori(0, B) as b:
                    sp.wait_ge(g["stored"], 16 * (b + 1))
                    sp.dma_start(g_ctx[:], ctx[bass.ds(b, 1), 0:S, :].rearrange("o (t p) d -> p (o t) d", p=P)
                                 ).then_inc(g["ctx_in"], 16)
                    sp.dma_start(r_x[:].rearrange("p j d -> p (j d)"),
                                 x[bass.ds(b, 1)].rearrange("o (p j) d -> p (o j d)", p=P)).then_inc(g["x_in"], 16)
                    sp.wait_ge(g["out"], b + 1)
                    sp.dma_start(out[bass.ds(b, 1)].rearrange("o (p j) d -> p (o j d)", p=P),
                                 g_n[:].rearrange("p j d -> p (j d)")).then_inc(g["stored"], 16)
                sp.wait_ge(g["stored"], 16 * (B + 1))
                sp.nop()
            sp.nop()

        @block.scalar
        def _(act):
            act.dma_start(gates[:, 0:1], g_x.to_broadcast([P, 1])).then_inc(s["g_in"], 16)
            act.dma_start(gates[:, 1:2], g_f.to_broadcast([P, 1])).then_inc(s["g_in"], 16)
            act.dma_start(w1_raw[:], w_in_t.rearrange("(k p) e -> p k e", p=P)).then_inc(s["w_in"], 16)
            act.dma_start(gres_sb[:], g_res).then_inc(s["w_in"], 16)
            act.dma_start(v_sb[:], v_t).then_inc(s["v_done"], 16)
            act.dma_start(c_sb[:], c_t).then_inc(s["v_done"], 16)
            act.dma_start(w2_raw[:], w_t.rearrange("(k p) e -> p k e", p=P)).then_inc(s["v_done"], 16)
            act.dma_start(ginit_b[:], g_init[0:1, 0:D].to_broadcast([P, D])).then_inc(s["b_scaled"], 16)
            act.dma_start(b1_b[:], b_in.to_broadcast([P, D])).then_inc(s["b_scaled"], 16)
            act.dma_start(b2_b[:], b_f.to_broadcast([P, D])).then_inc(s["b_scaled"], 16)
            act.wait_ge(s["g_in"], 32)
            nc.scalar.activation(tg[:], gates[:], ACT.Tanh).then_inc(s["tanh_done"], 1)

            def ctx_norm(b, q):
                act.wait_ge(ctx_in[q], 16 * (b // 2 + 1) if isinstance(b, int) else 8 * (b - q) + 16)
                wait(act, "ctx_r", b - 1)
                nc.scalar.activation(ctx_sq[:], ctx_sb[:, q, :], ACT.Square,
                                     accum_out=c_ss[:, q:q + 1]).then_inc(s["ctx_sqd"], 1)
                wait(act, "ctx_sqd", b + 1)
                nc.scalar.activation(c_std[:, q:q + 1], c_ss[:, q:q + 1], ACT.Sqrt, bias=con[:, C_Q + 1:C_Q + 2],
                                     scale=1.0 / DG).then_inc(s["ctx_std"], 1)

            def root1(i, q, h):
                wait(act, "stats1", i + 1)
                nc.scalar.activation(std1[:, q, h, :], mv1[:, q, h, :, 1], ACT.Sqrt, bias=con[:, C_Q + 2:C_Q + 3],
                                     scale=1.0 + EPS).then_inc(s["std1_s"], 1)

            def normalise(i, q, h):
                wait(act, "s1_done", i + 1)
                for j in (0, 1):
                    last = nc.scalar.activation(xn_sb[:, h, j, :], x_sb[:, q, h, j, :], ACT.Identity,
                                                bias=m1[:, q, h, j:j + 1], scale=s1[:, q, h, j:j + 1])
                last.then_inc(s["xn_done"], 1)

            def scale_ctx(b, q):
                wait(act, "ctx_r", b + 1)
                wait(act, "dp_mm", b)
                nc.scalar.activation(u_sb[:], ctx_sb[:, q, 0:D], ACT.Copy, scale=c_r[:, q:q + 1]).then_inc(s["u_done"], 1)

            def root2(i, q, h):
                wait(act, "stats2", i + 1)
                nc.scalar.activation(std2[:, q, h, :], mv2[:, q, h, :, 1], ACT.Sqrt,
                                     bias=con[:, C_Q + 1:C_Q + 2]).then_inc(s["std2_s"], 1)

            def split(i, h, bank, high, low, mm, hi_sem, lo_mm, lo_sem, part):
                if part == 0:
                    wait(act, mm, i + 1)
                    nc.scalar.copy(high[:, h], bank[:]).then_inc(s[hi_sem], 1)
                else:
                    wait(act, lo_mm, i + 1)
                    nc.scalar.copy(low[:, h], bank[:]).then_inc(s[lo_sem], 1)

            def split1(i, h, part):
                split(i, h, t1_ps, xt_hi, xt_lo, "t1_done", "hi1", "lo1_mm", "lo1", part)

            def split2(i, h, part):
                split(i, h, t2_ps, x1t_hi, x1t_lo, "t2_done", "hi2", "lo2_mm", "lo2", part)

            def dp_high(b, q):
                wait(act, "dpf_done", b + 1)
                nc.scalar.copy(dp_hi[:, q, :], dp_f[:]).then_inc(s["dph_done"], 1)

            act.wait_ge(s["con_in"], 32)
            root1(0, 0, 0)
            root1(1, 0, 1)
            normalise(0, 0, 0)
            act.wait_ge(s["w1_ready"], 1)
            nc.scalar.copy(w1_hi[:], w1_f[:]).then_inc(s["w1_hi_ready"], 1)
            nc.scalar.mul(neg_ident[:], ident, -1.0).then_inc(s["w1_hi_ready"], 1)
            ctx_norm(0, 0)
            split1(0, 0, 0)
            split1(0, 0, 1)
            scale_ctx(0, 0)
            normalise(1, 0, 1)
            dp_high(0, 0)
            act.wait_ge(s["w2_cen"], 1)
            nc.scalar.copy(w2_hi[:], w2_f[:]).then_inc(s["w2_hi_ready"], 1)

            def step(b, q, first=False, last=False, over=False):
                i = 2 * b
                r = 1 - q
                for h in (0, 1):
                    nq, nh = (q, 1) if h == 0 else (r, 0)
                    pq, ph = (r, 1) if h == 0 else (q, 0)
                    has_next = not over and not (last and h == 1)
                    if has_next:
                        split1(i + h + 1, nh, 0)
                    if not over and not last:
                        root1(i + h + 2, r, h)
                    if h == 0 and not over and not last:
                        ctx_norm(b + 1, r)
                    if has_next:
                        split1(i + h + 1, nh, 1)
                    if not (first and h == 0) and not (over and h == 1):
                        root2(i + h - 1, pq, ph)
                        split2(i + h - 1, ph, 0)
                    if not over and not last:
                        normalise(i + h + 2, r, h)
                    if not (first and h == 0) and not (over and h == 1):
                        split2(i + h - 1, ph, 1)
                    if h == 0 and not over and not last:
                        scale_ctx(b + 1, r)
                    if h == 1 and not over and not last:
                        dp_high(b + 1, r)

            step(0, 0, first=True)
            with act.Fori(0, 3) as k:
                step(2 * k + 1, 1)
                step(2 * k + 2, 0)
            step(7, 1, last=True)
            step(8, 0, over=True)

            with act.If(flagged(act)):
                with act.Fori(0, B) as b:
                    act.wait_ge(g["ctx_in"], 16 * (b + 1))
                    for t in range(QT):
                        last = nc.scalar.activation(ctx_sq[:], g_ctx[:, t, :], ACT.Square, accum_out=g_ss[:, t:t + 1])
                        last.then_inc(g["squared"], 1)
                        act.wait_ge(g["squared"], QT * b + t + 1)
                    nc.scalar.activation(g_std[:], g_ss[:], ACT.Sqrt, bias=con[:, C_Q + 1:C_Q + 2],
                                         scale=1.0 / DG).then_inc(g["ctx_std"], 1)
                    act.wait_ge(g["mv1"], b + 1)
                    act.wait_ge(g["ctx_inv"], b + 1)
                    nc.scalar.activation(g_std[:], g_mv[:, :, 1], ACT.Sqrt, bias=con[:, C_Q + 2:C_Q + 3],
                                         scale=1.0 + EPS).then_inc(g["std1"], 1)
                    act.wait_ge(g["mv2"], b + 1)
                    nc.scalar.activation(g_std[:], g_mv[:, :, 1], ACT.Sqrt,
                                         bias=con[:, C_Q + 1:C_Q + 2]).then_inc(g["std2"], 1)
                act.nop()
            act.nop()

        @block.vector
        def _(dve):
            V = nc.vector

            def stats(src, bn, mv, aggr_sem, done, i):
                V.bn_stats(bn[:, 0, :], src[:, 0, :])
                V.bn_stats(bn[:, 1, :], src[:, 1, :]).then_inc(s[aggr_sem], 1)
                wait_apart(dve, aggr_sem, i + 1)
                V.bn_aggr(mv[:, 0, :], bn[:, 0, :])
                V.bn_aggr(mv[:, 1, :], bn[:, 1, :]).then_inc(s[done], 1)

            def stats1(i, q, h):
                dve.wait_ge(x_in[q][h], 16 * (i // 4 + 1) if isinstance(i, int) else 4 * (i - (2 * q + h)) + 16)
                wait(dve, "xn_done", i - 3)
                stats(x_sb[:, q, h], bn1[:, q, h], mv1[:, q, h], "aggr1", "stats1", i)

            def recip1(i, q, h):
                wait(dve, "std1_s", i + 1)
                V.reciprocal(s1[:, q, h, :], std1[:, q, h, :]).then_inc(s["inv1"], 1)
                wait(dve, "inv1", i + 1)
                V.scalar_tensor_tensor(out=m1[:, q, h, :], in0=mv1[:, q, h, :, 0], scalar=-1.0, in1=s1[:, q, h, :],
                                       op0=ALU.mult, op1=ALU.mult).then_inc(s["s1_done"], 1)

            def recip2(i, q, h):
                wait(dve, "std2_s", i + 1)
                V.reciprocal(s2[:, q, h, :], std2[:, q, h, :]).then_inc(s["s2_done"], 1)

            def residual(i, q, h):
                wait(dve, "a_done", i + 1)
                V.tensor_tensor(x1_sb[:, q, h], a_ps[h][:], x_sb[:, q, h], ALU.add).then_inc(s["x1_done"], 1)
                wait(dve, "x1_done", i + 1)
                stats(x1_sb[:, q, h], bn2[:, q, h], mv2[:, q, h], "aggr2", "stats2", i)

            def finish(i, q, h):
                wait(dve, "b_done", i + 1)
                wait(dve, "x1b_done", i + 1)
                wait(dve, "s2_done", i + 1)
                for j in (0, 1):
                    last = V.scalar_tensor_tensor(out=out_sb[:, q, h, j, :], in0=b_ps[h][:, j, :],
                                                  scalar=s2[:, q, h, j:j + 1], in1=out_sb[:, q, h, j, :],
                                                  op0=ALU.mult, op1=ALU.add)
                last.then_inc(s["out_done"], 1)

            def ctx_recip(b, q):
                wait(dve, "ctx_std", b + 1)
                V.reciprocal(c_r[:, q:q + 1], c_std[:, q:q + 1]).then_inc(s["ctx_r"], 1)

            def dp_gain(b, q):
                wait(dve, "dp_mm", b + 1)
                wait(dve, "dpf_done", b)
                V.tensor_tensor(dp_g[:], dp_ps[:, 0:D], ginit_b[:], ALU.mult).then_inc(s["dpg_done"], 1)

            def make_pick(b, q):
                wait(dve, "plug_mm", b + 1)
                wait(dve, "a_done", 2 * b - 2)
                V.tensor_scalar(pick[:, q].rearrange("p j t -> p (j t)"), plug_ps[:], q_index, None,
                                ALU.is_equal).then_inc(s["pick_done"], 1)

            V.memset(ones_s[:], 1.0).then_inc(s["scanned"], 1)
            dve.wait_ge(s["scanned"], 1)
            dve.wait_ge(s["lens_in"], 16)
            V.tensor_tensor_scan(ends[:], ones_s[0:B, :], lens[:], 0.0, ALU.mult, ALU.add).then_inc(s["scanned"], 1)
            stats1(0, 0, 0)
            dve.wait_ge(s["ends_t"], 1)
            V.tensor_scalar(wrap[:], ends_ps, 0.5, float(S), ALU.is_lt, ALU.mult).then_inc(s["idx_w"], 1)
            dve.wait_ge(s["idx_w"], 1)
            V.scalar_tensor_tensor(out=bidx[:], in0=ends_ps, scalar=-1.0, in1=wrap[:], op0=ALU.add,
                                   op1=ALU.add).then_inc(s["idx_w"], 1)
            dve.wait_ge(s["idx_w"], 2)
            V.tensor_scalar(bidx_i[:], bidx[:], -1.0, float(S), ALU.max, ALU.min).then_inc(s["idx_w"], 1)
            dve.wait_ge(s["idx_w"], 3)
            V.tensor_scalar(bhi_i[:], bidx_i[:], LO.bit_length() - 1, None, ALU.arith_shift_right).then_inc(s["idx_i"], 1)
            V.tensor_scalar(blo_i[:], bidx_i[:], LO - 1, None, ALU.bitwise_and).then_inc(s["idx_i"], 1)
            dve.wait_ge(s["idx_i"], 2)
            V.tensor_copy(bhi[:], bhi_i[:]).then_inc(s["idx_i"], 1)
            V.tensor_copy(blo[:], blo_i[:]).then_inc(s["idx_i"], 1)
            dve.wait_ge(s["idx_i"], 4)
            dve.wait_ge(s["iotas"], 1)
            V.tensor_tensor(hot_hi[:], bhi[:].unsqueeze(1).to_broadcast([P, HI, PT * B]), iota_hi[:],
                            ALU.is_equal)
            V.tensor_tensor(hot_lo[:], blo[:].unsqueeze(1).to_broadcast([P, LO, PT * B]), iota_hi[:, 0:LO, :],
                            ALU.is_equal).then_inc(s["hots"], 1)
            stats1(1, 0, 1)
            recip1(0, 0, 0)
            dve.wait_ge(s["w_in"], 32)
            dve.wait_ge(s["tanh_done"], 1)
            for k in range(KB):
                last = V.tensor_scalar(w1_f[:, k, :], w1_raw[:, k, :], gres_sb[:, k:k + 1], tg[:, 0:1], ALU.mult, ALU.mult)
            last.then_inc(s["w1_ready"], 1)
            dve.wait_ge(s["counted"], 1)
            V.tensor_scalar(bound[:], count_ps[0:HI, 0:B * LO], 1.0, None, ALU.min).then_inc(s["bound_r"], 1)
            dve.wait_ge(s["w1_hi_ready"], 1)
            V.tensor_tensor(w1_lo[:], w1_f[:], w1_hi[:].bitcast(F32), ALU.subtract).then_inc(s["w_split"], 1)
            dve.wait_ge(s["bound_tr"], 1)
            V.tensor_copy(bound_t[:], bound_ps).then_inc(s["bound_h"], 1)
            recip1(1, 0, 1)
            dve.wait_ge(s["prefixed"], 1)
            V.tensor_tensor_scan(row_scan[:], ones_s[:, 0:HI], total_ps, 0.0, ALU.mult, ALU.add).then_inc(s["rows_scanned"], 1)
            dve.wait_ge(s["rows_scanned"], 1)
            V.tensor_tensor(row_ex[:], row_scan[:], total_ps, ALU.subtract).then_inc(s["rows_ex"], 1)
            dve.wait_ge(s["rows_ex"], 1)
            V.tensor_tensor(count[:], row_ex[:], prefix_ps, ALU.add).then_inc(s["counts"], 1)
            dve.wait_ge(s["counts"], 1)
            V.tensor_scalar(plug[:], count[:], -1.0, 0.0, ALU.add, ALU.max).then_inc(s["plugs"], 1)
            V.tensor_scalar(beyond[:], count[:, HI - 1:HI], float(P), None, ALU.is_gt).then_inc(s["plugs"], 1)
            dve.wait_ge(s["plugs"], 2)
            V.tensor_tensor(plug_x[:].rearrange("p (j h a) -> p h a j", j=TPB, a=LO // TPB),
                            plug[:].unsqueeze(2).unsqueeze(3).to_broadcast([P, HI, LO // TPB, TPB]),
                            lo_eye.rearrange("p (a j) -> p a j", j=TPB).unsqueeze(1).to_broadcast([P, HI, LO // TPB, TPB]),
                            ALU.mult).then_inc(s["plug_xed"], 1)
            ctx_recip(0, 0)
            dve.wait_ge(s["v_done"], 48)
            dve.wait_ge(s["w2_corr"], 1)
            V.tensor_tensor(w2_f[:], w2_raw[:], corr_ps[:], ALU.add).then_inc(s["w2_full"], 1)
            dve.wait_ge(s["b_scaled"], 48)
            V.tensor_scalar(ginit_b[:], ginit_b[:], tg[:, 0:1], None, ALU.mult).then_inc(s["b_scaled"], 1)
            V.tensor_scalar(b1_b[:], b1_b[:], tg[:, 0:1], None, ALU.mult).then_inc(s["b_scaled"], 1)
            V.tensor_scalar(b2_b[:], b2_b[:], tg[:, 1:2], None, ALU.mult).then_inc(s["b_scaled"], 1)
            dve.wait_ge(s["b_scaled"], 51)
            make_pick(0, 0)
            dp_gain(0, 0)
            dve.wait_ge(s["w2_mean"], 1)
            for k in range(KB):
                last = V.tensor_tensor(w2_raw[:, k, :], w2_f[:, k, :], mean_ps, ALU.subtract)
            last.then_inc(s["w2_full"], 1)
            dve.wait_ge(s["w2_full"], 2)
            V.tensor_scalar(w2_f[:], w2_raw[:], tg[:, 1:2], None, ALU.mult).then_inc(s["w2_cen"], 1)
            dve.wait_ge(s["w2_hi_ready"], 1)
            V.tensor_tensor(w2_lo[:], w2_f[:], w2_hi[:].bitcast(F32), ALU.subtract).then_inc(s["w_split"], 1)
            dve.wait_ge(s["flag_mm"], 1)
            V.tensor_copy(flag[:], flag_ps).then_inc(s["flag_set"], 1)

            def step(b, q, first=False, last=False, over=False):
                i = 2 * b
                r = 1 - q
                for h in (0, 1):
                    pq, ph = (r, 1) if h == 0 else (q, 0)
                    if not over and not last:
                        stats1(i + h + 2, r, h)
                    if not over:
                        residual(i + h, q, h)
                    if h == 1 and not over and not last:
                        dp_gain(b + 1, r)
                        make_pick(b + 1, r)
                    if not over and not last:
                        recip1(i + h + 2, r, h)
                    if h == 0 and not over and not last:
                        ctx_recip(b + 1, r)
                    if not (first and h == 0) and not (over and h == 1):
                        recip2(i + h - 1, pq, ph)
                    if not first:
                        finish(i + h - 2, r, h)

            step(0, 0, first=True)
            with dve.Fori(0, 3) as k:
                step(2 * k + 1, 1)
                step(2 * k + 2, 0)
            step(7, 1, last=True)
            step(8, 0, over=True)

            def stats_of(src, bn_sem, mv_sem, b):
                for j in range(TPB):
                    last = V.bn_stats(g_bn[:, j, :], src[:, j, :])
                last.then_inc(g[bn_sem], 1)
                dve.wait_ge(g[bn_sem], b + 1)
                dve.sem_inc(s["carrier"], 1)
                for j in range(TPB):
                    last = V.bn_aggr(g_mv[:, j, :], g_bn[:, j, :])
                last.then_inc(g[mv_sem], 1)

            def read_transposed(mm, read, b):
                dve.wait_ge(g[mm], b + 1)
                V.tensor_copy(g_t[:, 0:2].rearrange("p a b c -> p (a b) c"), t1_ps[:])
                V.tensor_copy(g_t[:, 2:4].rearrange("p a b c -> p (a b) c"), t2_ps[:]).then_inc(g[read], 1)

            with dve.If(flagged(dve)):
                with dve.Fori(0, B) as b:
                    dve.wait_ge(g["ctx_std"], b + 1)
                    V.reciprocal(g_inv[:], g_std[:]).then_inc(g["ctx_inv"], 1)
                    dve.wait_ge(g["ctx_inv"], b + 1)
                    for t in range(QT):
                        last = V.scalar_tensor_tensor(out=g_u[:, t, :], in0=g_ctx[:, t, 0:D], scalar=g_inv[:, t:t + 1],
                                                      in1=ginit_b[:], op0=ALU.mult, op1=ALU.mult)
                    last.then_inc(g["u"], 1)
                    dve.wait_ge(g["x_in"], 16 * (b + 1))
                    stats_of(r_x, "bn1", "mv1", b)
                    dve.wait_ge(g["scanned"], b + 1)
                    for n in (0, 1):
                        last = V.tensor_tensor(g_dp[:, 2 * n:2 * n + 2, :], a_ps[n][:],
                                               b1_b[:].unsqueeze(1).to_broadcast([P, 2, D]), ALU.add)
                    last.then_inc(g["dp"], 1)
                    dve.wait_ge(g["spread"], b + 1)
                    for t in range(QT):
                        last = V.tensor_scalar(g_pick[:, t, :], plug_ps[:], float(-P * t), q_index, ALU.add, ALU.is_equal)
                    last.then_inc(g["picks"], 1)
                    dve.wait_ge(g["std1"], b + 1)
                    V.reciprocal(g_inv[:], g_std[:]).then_inc(g["inv1"], 1)
                    dve.wait_ge(g["inv1"], b + 1)
                    for j in range(TPB):
                        last = V.tensor_scalar(g_n[:, j, :], r_x[:, j, :], g_mv[:, j, 0:1], g_inv[:, j:j + 1],
                                               ALU.subtract, ALU.mult)
                    last.then_inc(g["xn"], 1)
                    read_transposed("t1", "t1_read", b)
                    dve.wait_ge(g["mixed"], b + 1)
                    for n in (0, 1):
                        last = V.tensor_tensor(g_x1[:, 2 * n:2 * n + 2, :], a_ps[n][:], r_x[:, 2 * n:2 * n + 2, :], ALU.add)
                    last.then_inc(g["x1"], 1)
                    dve.wait_ge(g["x1"], b + 1)
                    stats_of(g_x1, "bn2", "mv2", b)
                    read_transposed("t2", "t2_read", b)
                    dve.wait_ge(g["std2"], b + 1)
                    V.reciprocal(g_inv[:], g_std[:]).then_inc(g["inv2"], 1)
                    dve.wait_ge(g["inv2"], b + 1)
                    dve.wait_ge(g["product"], b + 1)
                    for j in range(TPB):
                        last = V.scalar_tensor_tensor(out=g_n[:, j, :], in0=b_ps[j // 2][:, j % 2, :],
                                                      scalar=g_inv[:, j:j + 1], in1=g_x1[:, j, :], op0=ALU.mult, op1=ALU.add)
                    last.then_inc(g["scaled"], 1)
                    dve.wait_ge(g["scaled"], b + 1)
                    V.tensor_tensor(g_n[:], g_n[:], b2_b[:].unsqueeze(1).to_broadcast([P, TPB, D]), ALU.add
                                    ).then_inc(g["out"], 1)
                dve.nop()
            dve.nop()

        @block.gpsimd
        def _(pool):
            G = nc.gpsimd
            G.iota(iota_hi[:], [[1, HI], [0, PT * B]], base=0, channel_multiplier=0,
                   allow_small_or_imprecise_dtypes=True).then_inc(s["iotas"], 1)
            G.memset(mean_w[:], 1.0 / D).then_inc(s["consts_made"], 1)
            for q in (0, 1):
                for h in (0, 1):
                    pool.sem_inc(out_free[q][h], 16)

            def add_bias(i, q, h):
                wait(pool, "x1_done", i + 1)
                pool.wait_ge(out_free[q][h], 16 * (i // 4 + 1) if isinstance(i, int) else 4 * (i - (2 * q + h)) + 16)
                G.tensor_tensor(out_sb[:, q, h], x1_sb[:, q, h], b2_b[:].unsqueeze(1).to_broadcast([P, 2, D]),
                                ALU.add).then_inc(s["x1b_done"], 1)

            def dp_bias(b):
                wait(pool, "dpg_done", b + 1)
                wait(pool, "dpl_done", b)
                G.tensor_tensor(dp_f[:], dp_g[:], b1_b[:], ALU.add).then_inc(s["dpf_done"], 1)

            def dp_low(b, q):
                wait(pool, "dph_done", b + 1)
                G.tensor_tensor(dp_lo[:, q, :], dp_f[:], dp_hi[:, q, :].bitcast(F32), ALU.subtract).then_inc(s["dpl_done"], 1)

            pool.wait_ge(s["b_scaled"], 51)
            dp_bias(0)
            dp_low(0, 0)

            def step(b, q, first=False, last=False, over=False):
                i = 2 * b
                r = 1 - q
                for h in (0, 1):
                    if h == 1 and not last:
                        dp_bias(b + 1)
                    if h == 1 and not last:
                        dp_low(b + 1, r)
                    add_bias(i + h, q, h)

            step(0, 0, first=True)
            with pool.Fori(0, 3) as k:
                step(2 * k + 1, 1)
                step(2 * k + 2, 0)
            step(7, 1, last=True)

        @block.tensor
        def _(pe):
            T = nc.tensor

            def transpose1(i, h):
                wait(pe, "xn_done", i + 1)
                wait(pe, "lo1", i)
                for j in (0, 1):
                    for k in range(KB):
                        last = T.matmul(t1_ps[:, 2 * j + k, :], xn_sb[:, h, j, k * P:(k + 1) * P], ident,
                                        is_transpose=True, start=(j + k == 0), stop=True, skip_group_check=True)
                last.then_inc(s["t1_done"], 1)

            def low1(i, h):
                wait(pe, "hi1", i + 1)
                T.matmul(t1_ps[:].rearrange("p a b -> p (a b)"), neg_ident[:], xt_hi[:, h].rearrange("p a b -> p (a b)"),
                         start=False, stop=True, skip_group_check=True).then_inc(s["lo1_mm"], 1)

            def transpose2(i, q, h):
                wait(pe, "x1_done", i + 1)
                wait(pe, "lo2", i)
                for j in (0, 1):
                    for k in range(KB):
                        last = T.matmul(t2_ps[:, 2 * j + k, :], x1_sb[:, q, h, j, k * P:(k + 1) * P], ident,
                                        is_transpose=True, start=(j + k == 0), stop=True, skip_group_check=True)
                last.then_inc(s["t2_done"], 1)

            def low2(i, h):
                wait(pe, "hi2", i + 1)
                T.matmul(t2_ps[:].rearrange("p a b -> p (a b)"), neg_ident[:], x1t_hi[:, h].rearrange("p a b -> p (a b)"),
                         start=False, stop=True, skip_group_check=True).then_inc(s["lo2_mm"], 1)

            def product(bank, j, xh, xl, wh, wl, first, stop):
                for k in range(KB):
                    for xs, ws in ((xh, wh), (xh, wl), (xl, wh)):
                        last = T.matmul(bank[:, j, :], xs[:, 2 * j + k, :], ws[:, k, :], start=first,
                                        stop=stop and k == KB - 1 and xs is xl, skip_group_check=True)
                        first = False
                return last

            def attend(i, b, q, h):
                wait(pe, "lo1", i + 1)
                wait(pe, "x1_done", i - 1)
                for j in (0, 1):
                    product(a_ps[h], j, xt_hi[:, h], xt_lo[:, h], w1_hi, w1_lo, j == 0, False)
                if h == 0:
                    wait(pe, "pick_done", b + 1)
                    wait(pe, "dpl_done", b + 1)
                for j in (0, 1):
                    for part in (dp_hi, dp_lo):
                        last = T.matmul(a_ps[h][:, j, :], pick[:, q, 2 * h + j, :], part[:, q, :], start=False,
                                        stop=j == 1 and part is dp_lo, skip_group_check=True)
                last.then_inc(s["a_done"], 1)

            def ffn(i, h):
                wait(pe, "lo2", i + 1)
                if isinstance(i, int):
                    wait(pe, "out_done", i - 1)
                for j in (0, 1):
                    last = product(b_ps[h], j, x1t_hi[:, h], x1t_lo[:, h], w2_hi, w2_lo, True, True)
                last.then_inc(s["b_done"], 1)

            def scan(b):
                wait(pe, "u_done", b + 1)
                wait(pe, "dpg_done", b)
                T.matmul(dp_ps[:, 0:D], decay_t, u_sb[:], start=True, stop=True).then_inc(s["dp_mm"], 1)

            def spread(b):
                wait(pe, "plug_xed", 1)
                wait(pe, "pick_done", b)
                pick_b = batch_pick[:, b:b + 1] if isinstance(b, int) else batch_pick[:, bass.ds(b, 1)]
                T.matmul(plug_ps[:], pick_b.to_broadcast([P, P]), plug_x[:], start=True, stop=True).then_inc(s["plug_mm"], 1)

            pe.wait_ge(s["con_in"], 32)
            pe.wait_ge(s["scanned"], 2)
            for j in range(PT):
                last = T.transpose(ends_ps[:, B * j:B * j + B], ends[:, j * P:(j + 1) * P], ident[0:B, 0:B])
            last.then_inc(s["ends_t"], 1)
            pe.wait_ge(s["v_done"], 48)
            for k in range(KB):
                last = T.matmul(corr_ps[:, k, :], v_sb[:, k * P:(k + 1) * P], c_sb[:], start=True, stop=True)
            last.then_inc(s["w2_corr"], 1)
            pe.wait_ge(s["hots"], 1)
            for b in range(B):
                for j in range(PT):
                    last = T.matmul(count_ps[0:HI, b * LO:(b + 1) * LO], hot_hi[:, :, B * j + b], hot_lo[:, :, B * j + b],
                                    start=(j == 0), stop=(j == PT - 1))
            last.then_inc(s["counted"], 1)
            pe.wait_ge(s["bound_r"], 1)
            T.transpose(bound_ps, bound[:], ident[0:HI, 0:HI]).then_inc(s["bound_tr"], 1)
            pe.wait_ge(s["bound_h"], 1)
            T.matmul(prefix_ps, batch_prefix, bound_t[:], start=True, stop=True)
            T.matmul(total_ps, batch_ones, bound_t[:], start=True, stop=True).then_inc(s["prefixed"], 1)
            transpose1(0, 0)
            spread(0)
            pe.wait_ge(s["w1_hi_ready"], 2)
            low1(0, 0)
            T.matmul(flag_ps, beyond[:], ones_s[:, 0:1], start=True, stop=True).then_inc(s["flag_mm"], 1)
            scan(0)
            pe.wait_ge(s["w2_full"], 1)
            pe.wait_ge(s["consts_made"], 1)
            for k in range(KB):
                last = T.matmul(mean_ps, mean_w[:], w2_f[:, k, :], start=(k == 0), stop=(k == KB - 1))
            last.then_inc(s["w2_mean"], 1)
            pe.wait_ge(s["w_split"], 2)

            def step(b, q, first=False, last=False, over=False):
                i = 2 * b
                r = 1 - q
                for h in (0, 1):
                    nh = 1 - h
                    pq, ph = (r, 1) if h == 0 else (q, 0)
                    has_next = not over and not (last and h == 1)
                    if has_next:
                        transpose1(i + h + 1, nh)
                    if not over:
                        attend(i + h, b, q, h)
                    if has_next:
                        low1(i + h + 1, nh)
                    if h == 1 and not over and not last:
                        spread(b + 1)
                        scan(b + 1)
                    if not (first and h == 0) and not (over and h == 1):
                        transpose2(i + h - 1, pq, ph)
                    if not first:
                        ffn(i + h - 2, h)
                    if not (first and h == 0) and not (over and h == 1):
                        low2(i + h - 1, ph)

            step(0, 0, first=True)
            with pe.Fori(0, 3) as k:
                step(2 * k + 1, 1)
                step(2 * k + 2, 0)
            step(7, 1, last=True)
            step(8, 0, over=True)

            def transposed(src, j, bank):
                for k in range(KB):
                    last = T.transpose(bank[:, 2 * (j % 2) + k, :], src[:, j, k * P:(k + 1) * P], ident)
                return last

            with pe.If(flagged(pe)):
                with pe.Fori(0, B) as b:
                    pe.wait_ge(g["u"], b + 1)
                    for t in range(QT):
                        last = T.matmul(a_ps[t // 2][:, t % 2, :], decay_t, g_u[:, t, :], start=True, stop=t == 0)
                        if t:
                            last = T.matmul(a_ps[t // 2][:, t % 2, :], con[:, C_CORN:C_CORN + P], g_u[:, t - 1, :],
                                            start=False, stop=True)
                    last.then_inc(g["scanned"], 1)
                    T.matmul(plug_ps[:], batch_pick[:, bass.ds(b, 1)].to_broadcast([P, P]), plug_x[:], start=True,
                             stop=True).then_inc(g["spread"], 1)
                    pe.wait_ge(g["xn"], b + 1)
                    for j in range(TPB):
                        last = transposed(g_n, j, (t1_ps, t2_ps)[j // 2])
                    last.then_inc(g["t1"], 1)
                    pe.wait_ge(g["t1_read"], b + 1)
                    pe.wait_ge(g["picks"], b + 1)
                    pe.wait_ge(g["dp"], b + 1)
                    for j in range(TPB):
                        bank = a_ps[j // 2][:, j % 2, :]
                        for k in range(KB):
                            T.matmul(bank, g_t[:, j, k, :], w1_f[:, k, :], start=k == 0, stop=False)
                        for t in range(QT):
                            last = T.matmul(bank, g_pick[:, t, j * P:(j + 1) * P], g_dp[:, t, :], start=False, stop=t == QT - 1)
                    last.then_inc(g["mixed"], 1)
                    pe.wait_ge(g["x1"], b + 1)
                    for j in range(TPB):
                        last = transposed(g_x1, j, (t1_ps, t2_ps)[j // 2])
                    last.then_inc(g["t2"], 1)
                    pe.wait_ge(g["t2_read"], b + 1)
                    for j in range(TPB):
                        for k in range(KB):
                            last = T.matmul(b_ps[j // 2][:, j % 2, :], g_t[:, j, k, :], w2_f[:, k, :], start=k == 0,
                                            stop=k == KB - 1)
                    last.then_inc(g["product"], 1)
                pe.nop()
            pe.nop()


def shape_constants():
    n = np.arange(P)
    lag = n[None, :] - n[:, None]
    power = np.exp(-DT * np.maximum(lag, 0)) * np.exp(-EPS_DT)
    corner = np.exp(-DT * (lag + P)) * np.exp(-EPS_DT)
    con = np.zeros((P, C_END), np.float32)
    con[:, C_ID:C_ID + P] = np.eye(P)
    con[:, C_DEC:C_DEC + P] = np.where(lag >= 0, power, 0)
    con[:, C_CORN:C_CORN + P] = corner
    con[:, C_LO:C_LO + LO] = (n[:, None] % LO) == np.arange(LO)[None, :]
    con[:, C_Q] = n
    con[:, C_Q + 1] = EPS
    con[:, C_Q + 2] = EPS * EPS
    same = (n[:, None] // LO) == (n[None, :] // LO)
    msk = np.zeros((P, 2 * P + B), np.float16)
    msk[:, 0:P] = same & (n[:, None] <= n[None, :])
    msk[:, P:2 * P] = same
    msk[:, 2 * P:] = (n[:, None] // LO) == np.arange(B)[None, :]
    return con, msk


def kernel(x, ctx_2048, mask_BxS2_if0, g_xattn, g_ffn, L0_xattn_W_in, L0_xattn_b_in, L0_xattn_g_res,
           L0_xattn_g_init, L0_ffn_W, L0_ffn_b, L0_ffn_V_r, L0_ffn_C):
    import concourse.bacc as bacc
    from concourse.bass_utils import run_bass_kernel_spmd

    con, msk = shape_constants()
    laid = {
        "x": np.asarray(x),
        "ctx": np.asarray(ctx_2048),
        "mask": np.asarray(mask_BxS2_if0),
        "g_x": np.asarray(g_xattn).reshape(1, 1),
        "g_f": np.asarray(g_ffn).reshape(1, 1),
        "w_in_t": np.asarray(L0_xattn_W_in).T,
        "b_in": np.asarray(L0_xattn_b_in).reshape(1, D),
        "g_res": np.asarray(L0_xattn_g_res).reshape(KB, P).T,
        "g_init": np.asarray(L0_xattn_g_init).reshape(1, DG),
        "w_t": np.asarray(L0_ffn_W).T,
        "b_f": np.asarray(L0_ffn_b).reshape(1, D),
        "v_t": np.asarray(L0_ffn_V_r).T,
        "c_t": np.asarray(L0_ffn_C).T,
        "consts": con,
        "masks": msk,
    }
    nc = bacc.Bacc("TRN2", target_bir_lowering=False, num_devices=1)
    arrays, args = {}, []
    for name, a in laid.items():
        a = np.ascontiguousarray(a)
        arrays[f"in_{name}"] = a
        args.append(nc.dram_tensor(f"in_{name}", a.shape, mybir.dt.from_np(a.dtype), kind="ExternalInput").ap())
    out = nc.dram_tensor("out_x", (B, S, D), F32, kind="ExternalOutput").ap()
    build_gated_depool_ffn(nc, *args, out)
    r = run_bass_kernel_spmd(nc, [arrays], core_ids=[0])
    return r.results[0]["out_x"]
```

```python
from contextlib import ExitStack

import concourse.bass as bass
import numpy as np
from concourse import mybir

F32 = mybir.dt.float32
F32R = mybir.dt.float32r
F16 = mybir.dt.float16
BF16 = mybir.dt.bfloat16
I32 = mybir.dt.int32
ALU = mybir.AluOpType
ACT = mybir.ActivationFunctionType

B, S, D = 8, 512, 256
NP, DG = 1024, 512
R = 32
P = 128
KB = D // P
TPB = S // P
NPAIR = 2 * B
QT = S // P
EPS = 1e-5
LO = 16
HI = S // LO
PT = NP // P
EPS_DT = 0.001
DT = -np.log(-np.expm1(-EPS_DT))
C_DEC, C_CORN, C_LO, C_Q, C_END = 0, 128, 256, 272, 276
F_W, F_G, F_GATE, F_END = 0, KB * D, KB * D + KB, KB * D + KB + 2
S_W, S_GI, S_B1, S_B2, S_END = 0, KB * D, KB * D + D, KB * D + 2 * D, KB * D + 3 * D


def build_gated_depool_ffn(nc: bass.Bass, x, ctx, mask, first, second, ranks, consts, masks, out):
    es = ExitStack()
    with es:
        def sb(name, shape, dt=F32):
            return es.enter_context(nc.sbuf_tensor(name, shape, dt))

        def ps(name, shape):
            return es.enter_context(nc.psum_tensor(name, shape, F32))

        def sem(name):
            return es.enter_context(nc.semaphore(name))

        con = sb("con", [P, C_END])
        msk = sb("msk", [P, 2 * P + B], F16)
        decay_t = con[:, C_DEC:C_DEC + P]
        lo_eye = con[:, C_LO:C_LO + LO]
        q_index = con[:, C_Q:C_Q + 1]
        batch_prefix, batch_ones, batch_pick = msk[:, 0:P], msk[:, P:2 * P], msk[:, 2 * P:]
        ident = sb("ident", [P, P])
        neg_ident = sb("neg_ident", [P, P], F32R)
        first_sb = sb("first_sb", [P, F_END])
        second_sb = sb("second_sb", [P, S_END])
        ranks_sb = sb("ranks_sb", [R, 2 * D])
        mean_w = sb("mean_w", [P, P])
        tg = sb("tg", [P, 2])
        gates = first_sb[:, F_GATE:F_END]
        gres_sb = first_sb[:, F_G:F_GATE]
        w1_raw = first_sb[:, F_W:F_G].rearrange("p (k e) -> p k e", k=KB)
        w2_raw = second_sb[:, S_W:S_GI].rearrange("p (k e) -> p k e", k=KB)
        ginit_b = second_sb[:, S_GI:S_B1]
        b1_b = second_sb[:, S_B1:S_B2]
        b2_b = second_sb[:, S_B2:S_END]
        v_sb, c_sb = ranks_sb[:, 0:D], ranks_sb[:, D:2 * D]
        w1_f = sb("w1_f", [P, KB, D])
        w1_hi = sb("w1_hi", [P, KB, D], F32R)
        w1_lo = sb("w1_lo", [P, KB, D], F32R)
        w2_c = sb("w2_c", [P, KB, D])
        w2_f = sb("w2_f", [P, KB, D])
        w2_hi = sb("w2_hi", [P, KB, D], F32R)
        w2_lo = sb("w2_lo", [P, KB, D], F32R)
        lens = sb("lens", [B, NP], I32)
        one = sb("one", [P, 1])
        ends = sb("ends", [B, NP])
        wrap = sb("wrap", [P, PT * B])
        bidx = sb("bidx", [P, PT * B])
        bidx_i = sb("bidx_i", [P, PT * B], I32)
        bhi_i = sb("bhi_i", [P, PT * B], I32)
        blo_i = sb("blo_i", [P, PT * B], I32)
        bhi = sb("bhi", [P, PT * B], BF16)
        blo = sb("blo", [P, PT * B], BF16)
        iota_hi = sb("iota_hi", [P, HI, PT * B], BF16)
        hot_hi = sb("hot_hi", [P, HI, PT * B], BF16)
        hot_lo = sb("hot_lo", [P, LO, PT * B], BF16)
        bound = sb("bound", [HI, B * LO])
        bound_t = sb("bound_t", [P, HI], F16)
        row_scan = sb("row_scan", [P, HI])
        row_ex = sb("row_ex", [P, HI])
        count = sb("count", [P, HI])
        plug = sb("plug", [P, HI])
        plug_x = sb("plug_x", [P, S], F16)
        beyond = sb("beyond", [P, 1])
        flag = sb("flag", [1, 1], I32)
        x_sb = sb("x_sb", [P, 2, 2, 2, D])
        xn_sb = sb("xn_sb", [P, 2, 2, D])
        x1_sb = sb("x1_sb", [P, 2, 2, 2, D])
        out_sb = sb("out_sb", [P, 2, 2, 2, D])
        xt_hi = sb("xt_hi", [P, 2, 4, P], F32R)
        xt_lo = sb("xt_lo", [P, 2, 4, P], F32R)
        x1t_hi = sb("x1t_hi", [P, 2, 4, P], F32R)
        x1t_lo = sb("x1t_lo", [P, 2, 4, P], F32R)
        bn1 = sb("bn1", [P, 2, 2, 2, 6])
        mv1 = sb("mv1", [P, 2, 2, 2, 2])
        std1 = sb("std1", [P, 2, 2, 2])
        s1 = sb("s1", [P, 2, 2, 2])
        m1 = sb("m1", [P, 2, 2, 2])
        bn2 = sb("bn2", [P, 2, 2, 2, 6])
        mv2 = sb("mv2", [P, 2, 2, 2, 2])
        std2 = sb("std2", [P, 2, 2, 2])
        s2 = sb("s2", [P, 2, 2, 2])
        ctx_sb = sb("ctx_sb", [P, 2, DG])
        ctx_sq = sb("ctx_sq", [P, DG])
        c_ss = sb("c_ss", [P, 2])
        c_std = sb("c_std", [P, 2])
        c_r = sb("c_r", [P, 2])
        u_sb = sb("u_sb", [P, D])
        dp_g = sb("dp_g", [P, D])
        dp_f = sb("dp_f", [P, D])
        dp_hi = sb("dp_hi", [P, 2, D], F32R)
        dp_lo = sb("dp_lo", [P, 2, D], F32R)
        pick = sb("pick", [P, 2, TPB, P], F32R)

        g_ctx = sb("g_ctx", [P, QT, DG])
        g_ss = sb("g_ss", [P, QT])
        g_std = sb("g_std", [P, QT])
        g_inv = sb("g_inv", [P, QT])
        g_u = sb("g_u", [P, QT, D])
        g_dp = sb("g_dp", [P, QT, D])
        g_pick = sb("g_pick", [P, QT, S])
        r_x = sb("r_x", [P, TPB, D])
        g_n = sb("g_n", [P, TPB, D])
        g_t = sb("g_t", [P, TPB, KB, P])
        g_x1 = sb("g_x1", [P, TPB, D])
        g_bn = sb("g_bn", [P, TPB, 6])
        g_mv = sb("g_mv", [P, TPB, 2])

        t1_ps = ps("t1_ps", [P, 4, P])
        t2_ps = ps("t2_ps", [P, 4, P])
        a_ps = [ps(f"a_ps{n}", [P, 2, D]) for n in range(2)]
        b_ps = [ps(f"b_ps{n}", [P, 2, D]) for n in range(2)]
        dp_ps = ps("dp_ps", [P, 2 * D])
        plug_ps = ps("plug_ps", [P, S])
        ends_ps = t1_ps[:].rearrange("p a b -> p (a b)")[:, 0:PT * B]
        count_ps = t2_ps[:].rearrange("p a b -> p (a b)")
        bound_ps = dp_ps[:, 0:HI]
        prefix_ps = plug_ps[:, 0:HI]
        total_ps = plug_ps[:, 256:256 + HI]
        corr_ps = b_ps[0]
        mean_ps = b_ps[1][:, 0, :]
        flag_ps = b_ps[0][0:1, 0, 0:1]

        x_v = x.rearrange("b (p h j) d -> b p h (j d)", p=P, h=2)
        out_v = out.rearrange("b (p h j) d -> b p h (j d)", p=P, h=2)

        names = ("lens_in", "w_in", "con_in", "g_in", "iotas", "consts_made", "v_done", "ends_t", "scanned",
                 "hots", "counted", "bound_r", "bound_tr", "bound_h", "prefixed", "rows_scanned", "rows_ex", "counts", "plugs", "plug_xed",
                 "flag_mm", "flag_set", "tanh_done", "w1_ready", "w1_hi_ready", "w2_corr", "w2_full", "w2_mean", "w2_cen", "w2_hi_ready",
                 "w_split", "b_scaled",
                 "t1_done", "hi1", "lo1_mm", "lo1", "a_done", "x1_done", "t2_done", "hi2", "lo2_mm", "lo2", "b_done",
                 "stats1", "std1_s", "s1_done", "xn_done", "stats2", "std2_s", "s2_done", "x1b_done", "out_done",
                 "ctx_sqd", "ctx_std", "ctx_r", "u_done", "dp_mm", "dpg_done", "dpf_done", "dph_done", "dpl_done",
                 "plug_mm", "pick_done", "aggr1", "aggr2", "idx", "ident_made", "v_in", "w1_split", "w2_split", "carrier", "inv1")
        s = {n: sem(n) for n in names}
        x_in = [[sem(f"x_in{q}{h}") for h in range(2)] for q in range(2)]
        ctx_in = [sem(f"ctx_in{q}") for q in range(2)]
        out_free = [[sem(f"out_free{q}{h}") for h in range(2)] for q in range(2)]

        g = {n: sem("g_" + n) for n in (
            "stored", "ctx_in", "x_in", "squared", "ctx_std", "ctx_inv", "u", "scanned", "dp", "spread", "picks",
            "bn1", "mv1", "std1", "inv1", "xn", "t1", "t1_read", "mixed", "x1", "bn2", "mv2", "std2", "inv2",
            "t2", "t2_read", "product", "scaled", "out")}

        block = es.enter_context(nc.Block())

        def flagged(eng):
            eng.wait_ge(s["flag_set"], 1)
            return eng.value_load(flag[0:1, 0:1], min_val=0, max_val=P) > 0

        def wait(eng, name, value):
            if isinstance(value, int) and value <= 0:
                return
            eng.wait_ge(s[name], value)

        def wait_apart(eng, name, value):
            wait(eng, name, value)
            if not isinstance(value, int):
                eng.sem_inc(s["carrier"], 1)

        @block.sync
        def _(sp):
            sp.dma_start(lens[:], mask).then_inc(s["lens_in"], 16)

            def load_x(b, q, h):
                sp.dma_start(x_sb[:, q, h, :, :].rearrange("p j d -> p (j d)"), x_v[b, :, h, :]).then_inc(x_in[q][h], 16)

            def load_ctx(b, q):
                sp.dma_start(ctx_sb[:, q, :], ctx[b, 0:P, :]).then_inc(ctx_in[q], 16)

            load_x(0, 0, 0)
            sp.dma_start(con[:], consts).then_inc(s["con_in"], 16)
            load_x(0, 0, 1)
            load_ctx(0, 0)
            load_x(1, 1, 0)
            load_x(1, 1, 1)
            load_ctx(1, 1)

            def step(b, q, load, store):
                i = 2 * b
                for h in (0, 1):
                    if load:
                        wait(sp, "x1_done", i + h + 1)
                        load_x(b + 2, q, h)
                        if h == 0:
                            wait(sp, "u_done", b + 1)
                            load_ctx(b + 2, q)
                    if store:
                        wait(sp, "out_done", i + h - 1)
                        sp.dma_start(out_v[b - 1, :, h, :], out_sb[:, 1 - q, h, :, :].rearrange("p j d -> p (j d)")
                                     ).then_inc(out_free[1 - q][h], 16)

            step(0, 0, True, False)
            with sp.Fori(0, 2) as k:
                step(2 * k + 1, 1, True, True)
                step(2 * k + 2, 0, True, True)
            step(5, 1, True, True)
            for b in (6, 7, 8):
                step(b, b % 2, False, True)
            for q in (0, 1):
                for h in (0, 1):
                    sp.wait_ge(out_free[q][h], 16 * (B // 2 + 1))
            with sp.If(flagged(sp)):
                sp.sem_inc(g["stored"], 16)
                with sp.Fori(0, B) as b:
                    sp.wait_ge(g["stored"], 16 * (b + 1))
                    sp.dma_start(g_ctx[:], ctx[bass.ds(b, 1), 0:S, :].rearrange("o (t p) d -> p (o t) d", p=P)
                                 ).then_inc(g["ctx_in"], 16)
                    sp.dma_start(r_x[:].rearrange("p j d -> p (j d)"),
                                 x[bass.ds(b, 1)].rearrange("o (p j) d -> p (o j d)", p=P)).then_inc(g["x_in"], 16)
                    sp.wait_ge(g["out"], b + 1)
                    sp.dma_start(out[bass.ds(b, 1)].rearrange("o (p j) d -> p (o j d)", p=P),
                                 g_n[:].rearrange("p j d -> p (j d)")).then_inc(g["stored"], 16)
                sp.wait_ge(g["stored"], 16 * (B + 1))
                sp.nop()
            sp.nop()

        @block.scalar
        def _(act):
            act.dma_start(first_sb[:], first).then_inc(s["w_in"], 16)
            act.dma_start(msk[:], masks).then_inc(s["con_in"], 16)
            act.dma_start(ranks_sb[:], ranks).then_inc(s["v_in"], 16)
            act.dma_start(second_sb[:], second).then_inc(s["v_in"], 16)
            act.wait_ge(s["w_in"], 16)
            nc.scalar.activation(tg[:], gates, ACT.Tanh).then_inc(s["tanh_done"], 1)

            def ctx_norm(b, q):
                act.wait_ge(ctx_in[q], 16 * (b // 2 + 1) if isinstance(b, int) else 8 * (b - q) + 16)
                wait(act, "ctx_r", b - 1)
                nc.scalar.activation(ctx_sq[:], ctx_sb[:, q, :], ACT.Square,
                                     accum_out=c_ss[:, q:q + 1]).then_inc(s["ctx_sqd"], 1)
                wait(act, "ctx_sqd", b + 1)
                nc.scalar.activation(c_std[:, q:q + 1], c_ss[:, q:q + 1], ACT.Sqrt, bias=con[:, C_Q + 1:C_Q + 2],
                                     scale=1.0 / DG).then_inc(s["ctx_std"], 1)

            def root1(i, q, h):
                wait(act, "stats1", i + 1)
                nc.scalar.activation(std1[:, q, h, :], mv1[:, q, h, :, 1], ACT.Sqrt, bias=con[:, C_Q + 2:C_Q + 3],
                                     scale=1.0 + EPS).then_inc(s["std1_s"], 1)

            def normalise(i, q, h):
                wait(act, "s1_done", i + 1)
                for j in (0, 1):
                    last = nc.scalar.activation(xn_sb[:, h, j, :], x_sb[:, q, h, j, :], ACT.Identity,
                                                bias=m1[:, q, h, j:j + 1], scale=s1[:, q, h, j:j + 1])
                last.then_inc(s["xn_done"], 1)

            def scale_ctx(b, q):
                wait(act, "ctx_r", b + 1)
                wait(act, "dp_mm", b)
                nc.scalar.activation(u_sb[:], ctx_sb[:, q, 0:D], ACT.Copy, scale=c_r[:, q:q + 1]).then_inc(s["u_done"], 1)

            def root2(i, q, h):
                wait(act, "stats2", i + 1)
                nc.scalar.activation(std2[:, q, h, :], mv2[:, q, h, :, 1], ACT.Sqrt,
                                     bias=con[:, C_Q + 1:C_Q + 2]).then_inc(s["std2_s"], 1)

            def split(i, h, bank, high, low, mm, hi_sem, lo_mm, lo_sem, part):
                if part == 0:
                    wait(act, mm, i + 1)
                    nc.scalar.copy(high[:, h], bank[:]).then_inc(s[hi_sem], 1)
                else:
                    wait(act, lo_mm, i + 1)
                    nc.scalar.copy(low[:, h], bank[:]).then_inc(s[lo_sem], 1)

            def split1(i, h, part):
                split(i, h, t1_ps, xt_hi, xt_lo, "t1_done", "hi1", "lo1_mm", "lo1", part)

            def split2(i, h, part):
                split(i, h, t2_ps, x1t_hi, x1t_lo, "t2_done", "hi2", "lo2_mm", "lo2", part)

            def dp_high(b, q):
                wait(act, "dpf_done", b + 1)
                nc.scalar.copy(dp_hi[:, q, :], dp_f[:]).then_inc(s["dph_done"], 1)

            act.wait_ge(s["ident_made"], 1)
            nc.scalar.mul(neg_ident[:], ident[:], -1.0).then_inc(s["w1_hi_ready"], 1)
            act.wait_ge(s["con_in"], 32)
            root1(0, 0, 0)
            act.wait_ge(s["w1_ready"], 1)
            nc.scalar.copy(w1_hi[:], w1_f[:]).then_inc(s["w1_hi_ready"], 1)
            normalise(0, 0, 0)
            root1(1, 0, 1)
            split1(0, 0, 0)
            ctx_norm(0, 0)
            split1(0, 0, 1)
            normalise(1, 0, 1)
            scale_ctx(0, 0)
            dp_high(0, 0)

            def second_weights():
                act.wait_ge(s["w2_cen"], 1)
                nc.scalar.copy(w2_hi[:], w2_f[:]).then_inc(s["w2_hi_ready"], 1)

            def step(b, q, first=False, last=False, over=False):
                i = 2 * b
                r = 1 - q
                for h in (0, 1):
                    nq, nh = (q, 1) if h == 0 else (r, 0)
                    pq, ph = (r, 1) if h == 0 else (q, 0)
                    has_next = not over and not (last and h == 1)
                    has_prev = not (first and h == 0) and not (over and h == 1)
                    ahead = not over and not last
                    if has_next:
                        split1(i + h + 1, nh, 0)
                    if ahead:
                        root1(i + h + 2, r, h)
                    if h == 0 and ahead:
                        ctx_norm(b + 1, r)
                    if has_prev:
                        root2(i + h - 1, pq, ph)
                    if has_next:
                        split1(i + h + 1, nh, 1)
                    if has_prev:
                        split2(i + h - 1, ph, 0)
                    if ahead:
                        normalise(i + h + 2, r, h)
                    if has_prev:
                        split2(i + h - 1, ph, 1)
                    if h == 0 and ahead:
                        scale_ctx(b + 1, r)
                    if first and h == 0:
                        second_weights()
                    if h == 1 and ahead:
                        dp_high(b + 1, r)

            step(0, 0, first=True)
            with act.Fori(0, 3) as k:
                step(2 * k + 1, 1)
                step(2 * k + 2, 0)
            step(7, 1, last=True)
            step(8, 0, over=True)

            with act.If(flagged(act)):
                with act.Fori(0, B) as b:
                    act.wait_ge(g["ctx_in"], 16 * (b + 1))
                    for t in range(QT):
                        last = nc.scalar.activation(ctx_sq[:], g_ctx[:, t, :], ACT.Square, accum_out=g_ss[:, t:t + 1])
                        last.then_inc(g["squared"], 1)
                        act.wait_ge(g["squared"], QT * b + t + 1)
                    nc.scalar.activation(g_std[:], g_ss[:], ACT.Sqrt, bias=con[:, C_Q + 1:C_Q + 2],
                                         scale=1.0 / DG).then_inc(g["ctx_std"], 1)
                    act.wait_ge(g["mv1"], b + 1)
                    act.wait_ge(g["ctx_inv"], b + 1)
                    nc.scalar.activation(g_std[:], g_mv[:, :, 1], ACT.Sqrt, bias=con[:, C_Q + 2:C_Q + 3],
                                         scale=1.0 + EPS).then_inc(g["std1"], 1)
                    act.wait_ge(g["mv2"], b + 1)
                    nc.scalar.activation(g_std[:], g_mv[:, :, 1], ACT.Sqrt,
                                         bias=con[:, C_Q + 1:C_Q + 2]).then_inc(g["std2"], 1)
                act.nop()
            act.nop()

        @block.vector
        def _(dve):
            V = nc.vector

            def stats(src, bn, mv, aggr_sem, done, i):
                V.bn_stats(bn[:, 0, :], src[:, 0, :])
                V.bn_stats(bn[:, 1, :], src[:, 1, :]).then_inc(s[aggr_sem], 1)
                wait_apart(dve, aggr_sem, i + 1)
                V.bn_aggr(mv[:, 0, :], bn[:, 0, :])
                V.bn_aggr(mv[:, 1, :], bn[:, 1, :]).then_inc(s[done], 1)

            def stats1(i, q, h):
                dve.wait_ge(x_in[q][h], 16 * (i // 4 + 1) if isinstance(i, int) else 4 * (i - (2 * q + h)) + 16)
                wait(dve, "xn_done", i - 3)
                stats(x_sb[:, q, h], bn1[:, q, h], mv1[:, q, h], "aggr1", "stats1", i)

            def recip1(i, q, h):
                wait(dve, "std1_s", i + 1)
                V.reciprocal(s1[:, q, h, :], std1[:, q, h, :]).then_inc(s["inv1"], 1)
                wait(dve, "inv1", i + 1)
                V.scalar_tensor_tensor(out=m1[:, q, h, :], in0=mv1[:, q, h, :, 0], scalar=-1.0, in1=s1[:, q, h, :],
                                       op0=ALU.mult, op1=ALU.mult).then_inc(s["s1_done"], 1)

            def recip2(i, q, h):
                wait(dve, "std2_s", i + 1)
                V.reciprocal(s2[:, q, h, :], std2[:, q, h, :]).then_inc(s["s2_done"], 1)

            def residual(i, q, h):
                wait(dve, "a_done", i + 1)
                V.tensor_tensor(x1_sb[:, q, h], a_ps[h][:], x_sb[:, q, h], ALU.add).then_inc(s["x1_done"], 1)

            def stats2(i, q, h):
                wait(dve, "x1_done", i + 1)
                stats(x1_sb[:, q, h], bn2[:, q, h], mv2[:, q, h], "aggr2", "stats2", i)

            def finish(i, q, h):
                wait(dve, "b_done", i + 1)
                wait(dve, "x1b_done", i + 1)
                wait(dve, "s2_done", i + 1)
                for j in (0, 1):
                    last = V.scalar_tensor_tensor(out=out_sb[:, q, h, j, :], in0=b_ps[h][:, j, :],
                                                  scalar=s2[:, q, h, j:j + 1], in1=out_sb[:, q, h, j, :],
                                                  op0=ALU.mult, op1=ALU.add)
                last.then_inc(s["out_done"], 1)

            def ctx_recip(b, q):
                wait(dve, "ctx_std", b + 1)
                V.reciprocal(c_r[:, q:q + 1], c_std[:, q:q + 1]).then_inc(s["ctx_r"], 1)

            def dp_gain(b, q):
                wait(dve, "dp_mm", b + 1)
                wait(dve, "dpf_done", b)
                V.tensor_tensor(dp_g[:], dp_ps[:, 0:D], ginit_b, ALU.mult).then_inc(s["dpg_done"], 1)

            def make_pick(b, q):
                wait(dve, "plug_mm", b + 1)
                wait(dve, "a_done", 2 * b - 2)
                V.tensor_scalar(pick[:, q].rearrange("p j t -> p (j t)"), plug_ps[:], q_index, None,
                                ALU.is_equal).then_inc(s["pick_done"], 1)

            V.memset(one[:], 1.0).then_inc(s["scanned"], 1)
            dve.wait_ge(s["scanned"], 1)
            dve.wait_ge(s["lens_in"], 16)
            V.tensor_tensor_scan(ends[:], one[0:B, :].to_broadcast([B, NP]), lens[:], 0.0, ALU.mult, ALU.add
                                 ).then_inc(s["scanned"], 1)
            dve.wait_ge(s["ends_t"], 1)
            V.tensor_scalar(wrap[:], ends_ps, 0.5, float(S), ALU.is_lt, ALU.mult).then_inc(s["idx"], 1)
            dve.wait_ge(s["idx"], 1)
            V.scalar_tensor_tensor(out=bidx[:], in0=ends_ps, scalar=-1.0, in1=wrap[:], op0=ALU.add,
                                   op1=ALU.add).then_inc(s["idx"], 1)
            dve.wait_ge(s["idx"], 2)
            V.tensor_scalar(bidx_i[:], bidx[:], -1.0, float(S), ALU.max, ALU.min).then_inc(s["idx"], 1)
            dve.wait_ge(s["idx"], 3)
            V.tensor_scalar(bhi_i[:], bidx_i[:], LO.bit_length() - 1, None, ALU.arith_shift_right)
            V.tensor_scalar(blo_i[:], bidx_i[:], LO - 1, None, ALU.bitwise_and).then_inc(s["idx"], 1)
            dve.wait_ge(s["idx"], 4)
            V.tensor_copy(bhi[:], bhi_i[:])
            V.tensor_copy(blo[:], blo_i[:]).then_inc(s["idx"], 1)
            dve.wait_ge(s["idx"], 5)
            dve.wait_ge(s["iotas"], 1)
            V.tensor_tensor(hot_hi[:], bhi[:].unsqueeze(1).to_broadcast([P, HI, PT * B]), iota_hi[:],
                            ALU.is_equal)
            V.tensor_tensor(hot_lo[:], blo[:].unsqueeze(1).to_broadcast([P, LO, PT * B]), iota_hi[:, 0:LO, :],
                            ALU.is_equal).then_inc(s["hots"], 1)
            stats1(0, 0, 0)
            dve.wait_ge(s["tanh_done"], 1)
            for k in range(KB):
                last = V.tensor_scalar(w1_f[:, k, :], w1_raw[:, k, :], gres_sb[:, k:k + 1], tg[:, 0:1], ALU.mult, ALU.mult)
            last.then_inc(s["w1_ready"], 1)
            recip1(0, 0, 0)
            stats1(1, 0, 1)
            dve.wait_ge(s["counted"], 1)
            V.tensor_scalar(bound[:], count_ps[0:HI, 0:B * LO], 1.0, None, ALU.min).then_inc(s["bound_r"], 1)
            dve.wait_ge(s["w1_hi_ready"], 2)
            V.tensor_tensor(w1_lo[:], w1_f[:], w1_hi[:].bitcast(F32), ALU.subtract).then_inc(s["w1_split"], 1)
            dve.wait_ge(s["bound_tr"], 1)
            V.tensor_copy(bound_t[:], bound_ps).then_inc(s["bound_h"], 1)
            recip1(1, 0, 1)
            ctx_recip(0, 0)
            dve.wait_ge(s["prefixed"], 1)
            V.tensor_tensor_scan(row_scan[:], one[:].to_broadcast([P, HI]), total_ps, 0.0, ALU.mult, ALU.add
                                 ).then_inc(s["counts"], 1)
            dve.wait_ge(s["counts"], 1)
            V.tensor_tensor(row_ex[:], row_scan[:], total_ps, ALU.subtract).then_inc(s["counts"], 1)
            dve.wait_ge(s["counts"], 2)
            V.tensor_tensor(count[:], row_ex[:], prefix_ps, ALU.add).then_inc(s["counts"], 1)
            dve.wait_ge(s["counts"], 3)
            V.tensor_scalar(plug[:], count[:], -1.0, 0.0, ALU.add, ALU.max)
            V.tensor_scalar(beyond[:], count[:, HI - 1:HI], float(P), None, ALU.is_gt).then_inc(s["plugs"], 1)
            dve.wait_ge(s["plugs"], 1)
            V.tensor_tensor(plug_x[:].rearrange("p (j h a) -> p h a j", j=TPB, a=LO // TPB),
                            plug[:].unsqueeze(2).unsqueeze(3).to_broadcast([P, HI, LO // TPB, TPB]),
                            lo_eye.rearrange("p (a j) -> p a j", j=TPB).unsqueeze(1).to_broadcast([P, HI, LO // TPB, TPB]),
                            ALU.mult).then_inc(s["plug_xed"], 1)
            dve.wait_ge(s["v_in"], 32)
            V.tensor_scalar(ginit_b, ginit_b, tg[:, 0:1], None, ALU.mult).then_inc(s["b_scaled"], 1)
            V.tensor_scalar(b1_b, b1_b, tg[:, 0:1], None, ALU.mult)
            V.tensor_scalar(b2_b, b2_b, tg[:, 1:2], None, ALU.mult).then_inc(s["b_scaled"], 1)
            dve.wait_ge(s["b_scaled"], 1)
            dp_gain(0, 0)
            make_pick(0, 0)

            def second_weights(part):
                if part == 0:
                    dve.wait_ge(s["w2_corr"], 1)
                    V.tensor_tensor(w2_f[:], w2_raw, corr_ps[:], ALU.add).then_inc(s["w2_full"], 1)
                    return
                dve.wait_ge(s["flag_mm"], 1)
                V.tensor_copy(flag[:], flag_ps).then_inc(s["flag_set"], 1)
                dve.wait_ge(s["w2_mean"], 1)
                for k in range(KB):
                    last = V.tensor_tensor(w2_c[:, k, :], w2_f[:, k, :], mean_ps, ALU.subtract)
                last.then_inc(s["w2_full"], 1)
                dve.wait_ge(s["w2_full"], 2)
                V.tensor_scalar(w2_f[:], w2_c[:], tg[:, 1:2], None, ALU.mult).then_inc(s["w2_cen"], 1)
                dve.wait_ge(s["w2_hi_ready"], 1)
                V.tensor_tensor(w2_lo[:], w2_f[:], w2_hi[:].bitcast(F32), ALU.subtract).then_inc(s["w2_split"], 1)
            def step(b, q, first=False, last=False, over=False):
                i = 2 * b
                r = 1 - q
                for h in (0, 1):
                    pq, ph = (r, 1) if h == 0 else (q, 0)
                    has_prev = not (first and h == 0) and not (over and h == 1)
                    ahead = not over and not last
                    if ahead:
                        stats1(i + h + 2, r, h)
                    if first and h == 0:
                        second_weights(0)
                    if not over:
                        residual(i + h, q, h)
                    if ahead:
                        recip1(i + h + 2, r, h)
                    if not over:
                        stats2(i + h, q, h)
                    if h == 1 and ahead:
                        dp_gain(b + 1, r)
                        make_pick(b + 1, r)
                    if h == 0 and ahead:
                        ctx_recip(b + 1, r)
                    if first and h == 0:
                        second_weights(1)
                    if has_prev:
                        recip2(i + h - 1, pq, ph)
                    if not first:
                        finish(i + h - 2, r, h)

            step(0, 0, first=True)
            with dve.Fori(0, 3) as k:
                step(2 * k + 1, 1)
                step(2 * k + 2, 0)
            step(7, 1, last=True)
            step(8, 0, over=True)

            def stats_of(src, bn_sem, mv_sem, b):
                for j in range(TPB):
                    last = V.bn_stats(g_bn[:, j, :], src[:, j, :])
                last.then_inc(g[bn_sem], 1)
                dve.wait_ge(g[bn_sem], b + 1)
                dve.sem_inc(s["carrier"], 1)
                for j in range(TPB):
                    last = V.bn_aggr(g_mv[:, j, :], g_bn[:, j, :])
                last.then_inc(g[mv_sem], 1)

            def read_transposed(mm, read, b):
                dve.wait_ge(g[mm], b + 1)
                V.tensor_copy(g_t[:, 0:2].rearrange("p a b c -> p (a b) c"), t1_ps[:])
                V.tensor_copy(g_t[:, 2:4].rearrange("p a b c -> p (a b) c"), t2_ps[:]).then_inc(g[read], 1)

            with dve.If(flagged(dve)):
                with dve.Fori(0, B) as b:
                    dve.wait_ge(g["ctx_std"], b + 1)
                    V.reciprocal(g_inv[:], g_std[:]).then_inc(g["ctx_inv"], 1)
                    dve.wait_ge(g["ctx_inv"], b + 1)
                    for t in range(QT):
                        last = V.scalar_tensor_tensor(out=g_u[:, t, :], in0=g_ctx[:, t, 0:D], scalar=g_inv[:, t:t + 1],
                                                      in1=ginit_b, op0=ALU.mult, op1=ALU.mult)
                    last.then_inc(g["u"], 1)
                    dve.wait_ge(g["x_in"], 16 * (b + 1))
                    stats_of(r_x, "bn1", "mv1", b)
                    dve.wait_ge(g["scanned"], b + 1)
                    for n in (0, 1):
                        last = V.tensor_tensor(g_dp[:, 2 * n:2 * n + 2, :], a_ps[n][:],
                                               b1_b.unsqueeze(1).to_broadcast([P, 2, D]), ALU.add)
                    last.then_inc(g["dp"], 1)
                    dve.wait_ge(g["spread"], b + 1)
                    for t in range(QT):
                        last = V.tensor_scalar(g_pick[:, t, :], plug_ps[:], float(-P * t), q_index, ALU.add, ALU.is_equal)
                    last.then_inc(g["picks"], 1)
                    dve.wait_ge(g["std1"], b + 1)
                    V.reciprocal(g_inv[:], g_std[:]).then_inc(g["inv1"], 1)
                    dve.wait_ge(g["inv1"], b + 1)
                    for j in range(TPB):
                        last = V.tensor_scalar(g_n[:, j, :], r_x[:, j, :], g_mv[:, j, 0:1], g_inv[:, j:j + 1],
                                               ALU.subtract, ALU.mult)
                    last.then_inc(g["xn"], 1)
                    read_transposed("t1", "t1_read", b)
                    dve.wait_ge(g["mixed"], b + 1)
                    for n in (0, 1):
                        last = V.tensor_tensor(g_x1[:, 2 * n:2 * n + 2, :], a_ps[n][:], r_x[:, 2 * n:2 * n + 2, :], ALU.add)
                    last.then_inc(g["x1"], 1)
                    dve.wait_ge(g["x1"], b + 1)
                    stats_of(g_x1, "bn2", "mv2", b)
                    read_transposed("t2", "t2_read", b)
                    dve.wait_ge(g["std2"], b + 1)
                    V.reciprocal(g_inv[:], g_std[:]).then_inc(g["inv2"], 1)
                    dve.wait_ge(g["inv2"], b + 1)
                    dve.wait_ge(g["product"], b + 1)
                    for j in range(TPB):
                        last = V.scalar_tensor_tensor(out=g_n[:, j, :], in0=b_ps[j // 2][:, j % 2, :],
                                                      scalar=g_inv[:, j:j + 1], in1=g_x1[:, j, :], op0=ALU.mult, op1=ALU.add)
                    last.then_inc(g["scaled"], 1)
                    dve.wait_ge(g["scaled"], b + 1)
                    V.tensor_tensor(g_n[:], g_n[:], b2_b.unsqueeze(1).to_broadcast([P, TPB, D]), ALU.add
                                    ).then_inc(g["out"], 1)
                dve.nop()
            dve.nop()

        @block.gpsimd
        def _(pool):
            G = nc.gpsimd
            G.memset(ident[:], 0.0).then_inc(s["consts_made"], 1)
            pool.wait_ge(s["consts_made"], 1)
            G.affine_select(out=ident[:], in_=ident[:], compare_op=ALU.not_equal, fill=1.0, base=0,
                            pattern=[[-1, P]], channel_multiplier=1).then_inc(s["ident_made"], 1)
            G.iota(iota_hi[:], [[1, HI], [0, PT * B]], base=0, channel_multiplier=0,
                   allow_small_or_imprecise_dtypes=True).then_inc(s["iotas"], 1)
            G.memset(mean_w[:], 1.0 / D).then_inc(s["consts_made"], 1)
            for q in (0, 1):
                for h in (0, 1):
                    pool.sem_inc(out_free[q][h], 16)

            def add_bias(i, q, h):
                wait(pool, "x1_done", i + 1)
                pool.wait_ge(out_free[q][h], 16 * (i // 4 + 1) if isinstance(i, int) else 4 * (i - (2 * q + h)) + 16)
                G.tensor_tensor(out_sb[:, q, h], x1_sb[:, q, h], b2_b.unsqueeze(1).to_broadcast([P, 2, D]),
                                ALU.add).then_inc(s["x1b_done"], 1)

            def dp_bias(b):
                wait(pool, "dpg_done", b + 1)
                wait(pool, "dpl_done", b)
                G.tensor_tensor(dp_f[:], dp_g[:], b1_b, ALU.add).then_inc(s["dpf_done"], 1)

            def dp_low(b, q):
                wait(pool, "dph_done", b + 1)
                G.tensor_tensor(dp_lo[:, q, :], dp_f[:], dp_hi[:, q, :].bitcast(F32), ALU.subtract).then_inc(s["dpl_done"], 1)

            pool.wait_ge(s["b_scaled"], 2)
            dp_bias(0)
            dp_low(0, 0)

            def step(b, q, first=False, last=False, over=False):
                i = 2 * b
                r = 1 - q
                for h in (0, 1):
                    if h == 1 and not last:
                        dp_bias(b + 1)
                    if h == 1 and not last:
                        dp_low(b + 1, r)
                    add_bias(i + h, q, h)

            step(0, 0, first=True)
            with pool.Fori(0, 3) as k:
                step(2 * k + 1, 1)
                step(2 * k + 2, 0)
            step(7, 1, last=True)

        @block.tensor
        def _(pe):
            T = nc.tensor

            def transpose1(i, h):
                wait(pe, "xn_done", i + 1)
                wait(pe, "lo1", i)
                for j in (0, 1):
                    for k in range(KB):
                        last = T.matmul(t1_ps[:, 2 * j + k, :], xn_sb[:, h, j, k * P:(k + 1) * P], ident[:],
                                        is_transpose=True, start=(j + k == 0), stop=True, skip_group_check=True)
                last.then_inc(s["t1_done"], 1)

            def low1(i, h):
                wait(pe, "hi1", i + 1)
                T.matmul(t1_ps[:].rearrange("p a b -> p (a b)"), neg_ident[:], xt_hi[:, h].rearrange("p a b -> p (a b)"),
                         start=False, stop=True, skip_group_check=True).then_inc(s["lo1_mm"], 1)

            def transpose2(i, q, h):
                wait(pe, "x1_done", i + 1)
                wait(pe, "lo2", i)
                for j in (0, 1):
                    for k in range(KB):
                        last = T.matmul(t2_ps[:, 2 * j + k, :], x1_sb[:, q, h, j, k * P:(k + 1) * P], ident[:],
                                        is_transpose=True, start=(j + k == 0), stop=True, skip_group_check=True)
                last.then_inc(s["t2_done"], 1)

            def low2(i, h):
                wait(pe, "hi2", i + 1)
                T.matmul(t2_ps[:].rearrange("p a b -> p (a b)"), neg_ident[:], x1t_hi[:, h].rearrange("p a b -> p (a b)"),
                         start=False, stop=True, skip_group_check=True).then_inc(s["lo2_mm"], 1)

            def product(bank, j, xh, xl, wh, wl, first, stop):
                for k in range(KB):
                    for xs, ws in ((xh, wh), (xh, wl), (xl, wh)):
                        last = T.matmul(bank[:, j, :], xs[:, 2 * j + k, :], ws[:, k, :], start=first,
                                        stop=stop and k == KB - 1 and xs is xl, skip_group_check=True)
                        first = False
                return last

            def attend(i, b, q, h):
                wait(pe, "lo1", i + 1)
                wait(pe, "x1_done", i - 1)
                for j in (0, 1):
                    product(a_ps[h], j, xt_hi[:, h], xt_lo[:, h], w1_hi, w1_lo, j == 0, False)
                if h == 0:
                    wait(pe, "pick_done", b + 1)
                    wait(pe, "dpl_done", b + 1)
                for j in (0, 1):
                    for part in (dp_hi, dp_lo):
                        last = T.matmul(a_ps[h][:, j, :], pick[:, q, 2 * h + j, :], part[:, q, :], start=False,
                                        stop=j == 1 and part is dp_lo, skip_group_check=True)
                last.then_inc(s["a_done"], 1)

            def ffn(i, h):
                wait(pe, "lo2", i + 1)
                if isinstance(i, int):
                    wait(pe, "out_done", i - 1)
                for j in (0, 1):
                    last = product(b_ps[h], j, x1t_hi[:, h], x1t_lo[:, h], w2_hi, w2_lo, True, True)
                last.then_inc(s["b_done"], 1)

            def scan(b):
                wait(pe, "u_done", b + 1)
                wait(pe, "dpg_done", b)
                T.matmul(dp_ps[:, 0:D], decay_t, u_sb[:], start=True, stop=True).then_inc(s["dp_mm"], 1)

            def spread(b):
                wait(pe, "plug_xed", 1)
                wait(pe, "pick_done", b)
                pick_b = batch_pick[:, b:b + 1] if isinstance(b, int) else batch_pick[:, bass.ds(b, 1)]
                T.matmul(plug_ps[:], pick_b.to_broadcast([P, P]), plug_x[:], start=True, stop=True).then_inc(s["plug_mm"], 1)

            pe.wait_ge(s["ident_made"], 1)
            pe.wait_ge(s["scanned"], 2)
            for j in range(PT):
                last = T.transpose(ends_ps[:, B * j:B * j + B], ends[:, j * P:(j + 1) * P], ident[0:B, 0:B])
            last.then_inc(s["ends_t"], 1)
            pe.wait_ge(s["v_in"], 32)
            for k in range(KB):
                last = T.matmul(corr_ps[:, k, :], v_sb[:, k * P:(k + 1) * P], c_sb, start=True, stop=True)
            last.then_inc(s["w2_corr"], 1)
            pe.wait_ge(s["hots"], 1)
            for b in range(B):
                for j in range(PT):
                    last = T.matmul(count_ps[0:HI, b * LO:(b + 1) * LO], hot_hi[:, :, B * j + b], hot_lo[:, :, B * j + b],
                                    start=(j == 0), stop=(j == PT - 1))
            last.then_inc(s["counted"], 1)
            pe.wait_ge(s["bound_r"], 1)
            T.transpose(bound_ps, bound[:], ident[0:HI, 0:HI]).then_inc(s["bound_tr"], 1)
            transpose1(0, 0)
            pe.wait_ge(s["con_in"], 32)
            pe.wait_ge(s["bound_h"], 1)
            T.matmul(prefix_ps, batch_prefix, bound_t[:], start=True, stop=True)
            T.matmul(total_ps, batch_ones, bound_t[:], start=True, stop=True).then_inc(s["prefixed"], 1)
            low1(0, 0)
            scan(0)
            pe.wait_ge(s["w1_split"], 1)

            def second_weights():
                pe.wait_ge(s["w2_full"], 1)
                pe.wait_ge(s["consts_made"], 2)
                T.matmul(flag_ps, beyond[:], one[:], start=True, stop=True).then_inc(s["flag_mm"], 1)
                for k in range(KB):
                    last = T.matmul(mean_ps, mean_w[:], w2_f[:, k, :], start=(k == 0), stop=(k == KB - 1))
                last.then_inc(s["w2_mean"], 1)

            def step(b, q, first=False, last=False, over=False):
                i = 2 * b
                r = 1 - q
                for h in (0, 1):
                    nh = 1 - h
                    pq, ph = (r, 1) if h == 0 else (q, 0)
                    has_next = not over and not (last and h == 1)
                    if has_next:
                        transpose1(i + h + 1, nh)
                    if first and h == 0:
                        spread(0)
                    if not over:
                        attend(i + h, b, q, h)
                    if first and h == 0:
                        second_weights()
                    if has_next:
                        low1(i + h + 1, nh)
                    if h == 1 and not over and not last:
                        spread(b + 1)
                        scan(b + 1)
                    if not (first and h == 0) and not (over and h == 1):
                        transpose2(i + h - 1, pq, ph)
                    if not first:
                        if isinstance(b, int) and b == 1 and h == 0:
                            pe.wait_ge(s["w2_split"], 1)
                        ffn(i + h - 2, h)
                    if not (first and h == 0) and not (over and h == 1):
                        low2(i + h - 1, ph)

            step(0, 0, first=True)
            with pe.Fori(0, 3) as k:
                step(2 * k + 1, 1)
                step(2 * k + 2, 0)
            step(7, 1, last=True)
            step(8, 0, over=True)

            def transposed(src, j, bank):
                for k in range(KB):
                    last = T.transpose(bank[:, 2 * (j % 2) + k, :], src[:, j, k * P:(k + 1) * P], ident[:])
                return last

            with pe.If(flagged(pe)):
                with pe.Fori(0, B) as b:
                    pe.wait_ge(g["u"], b + 1)
                    for t in range(QT):
                        last = T.matmul(a_ps[t // 2][:, t % 2, :], decay_t, g_u[:, t, :], start=True, stop=t == 0)
                        if t:
                            last = T.matmul(a_ps[t // 2][:, t % 2, :], con[:, C_CORN:C_CORN + P], g_u[:, t - 1, :],
                                            start=False, stop=True)
                    last.then_inc(g["scanned"], 1)
                    T.matmul(plug_ps[:], batch_pick[:, bass.ds(b, 1)].to_broadcast([P, P]), plug_x[:], start=True,
                             stop=True).then_inc(g["spread"], 1)
                    pe.wait_ge(g["xn"], b + 1)
                    for j in range(TPB):
                        last = transposed(g_n, j, (t1_ps, t2_ps)[j // 2])
                    last.then_inc(g["t1"], 1)
                    pe.wait_ge(g["t1_read"], b + 1)
                    pe.wait_ge(g["picks"], b + 1)
                    pe.wait_ge(g["dp"], b + 1)
                    for j in range(TPB):
                        bank = a_ps[j // 2][:, j % 2, :]
                        for k in range(KB):
                            T.matmul(bank, g_t[:, j, k, :], w1_f[:, k, :], start=k == 0, stop=False)
                        for t in range(QT):
                            last = T.matmul(bank, g_pick[:, t, j * P:(j + 1) * P], g_dp[:, t, :], start=False, stop=t == QT - 1)
                    last.then_inc(g["mixed"], 1)
                    pe.wait_ge(g["x1"], b + 1)
                    for j in range(TPB):
                        last = transposed(g_x1, j, (t1_ps, t2_ps)[j // 2])
                    last.then_inc(g["t2"], 1)
                    pe.wait_ge(g["t2_read"], b + 1)
                    for j in range(TPB):
                        for k in range(KB):
                            last = T.matmul(b_ps[j // 2][:, j % 2, :], g_t[:, j, k, :], w2_f[:, k, :], start=k == 0,
                                            stop=k == KB - 1)
                    last.then_inc(g["product"], 1)
                pe.nop()
            pe.nop()


def shape_constants():
    n = np.arange(P)
    lag = n[None, :] - n[:, None]
    power = np.exp(-DT * np.maximum(lag, 0)) * np.exp(-EPS_DT)
    corner = np.exp(-DT * (lag + P)) * np.exp(-EPS_DT)
    con = np.zeros((P, C_END), np.float32)
    con[:, C_DEC:C_DEC + P] = np.where(lag >= 0, power, 0)
    con[:, C_CORN:C_CORN + P] = corner
    con[:, C_LO:C_LO + LO] = (n[:, None] % LO) == np.arange(LO)[None, :]
    con[:, C_Q] = n
    con[:, C_Q + 1] = EPS
    con[:, C_Q + 2] = EPS * EPS
    same = (n[:, None] // LO) == (n[None, :] // LO)
    msk = np.zeros((P, 2 * P + B), np.float16)
    msk[:, 0:P] = same & (n[:, None] <= n[None, :])
    msk[:, P:2 * P] = same
    msk[:, 2 * P:] = (n[:, None] // LO) == np.arange(B)[None, :]
    return con, msk


def kernel(x, ctx_2048, mask_BxS2_if0, g_xattn, g_ffn, L0_xattn_W_in, L0_xattn_b_in, L0_xattn_g_res,
           L0_xattn_g_init, L0_ffn_W, L0_ffn_b, L0_ffn_V_r, L0_ffn_C):
    import concourse.bacc as bacc
    from concourse.bass_utils import run_bass_kernel_spmd

    con, msk = shape_constants()
    def by_blocks(w):
        return np.asarray(w).T.reshape(KB, P, D).transpose(1, 0, 2).reshape(P, KB * D)

    def everywhere(v):
        v = np.asarray(v)
        return np.broadcast_to(v.reshape(1, v.size), (P, v.size))

    laid = {
        "x": np.asarray(x),
        "ctx": np.asarray(ctx_2048),
        "mask": np.asarray(mask_BxS2_if0),
        "first": np.concatenate([by_blocks(L0_xattn_W_in), np.asarray(L0_xattn_g_res).reshape(KB, P).T,
                                 everywhere(g_xattn), everywhere(g_ffn)], axis=1),
        "second": np.concatenate([by_blocks(L0_ffn_W), everywhere(L0_xattn_g_init)[:, 0:D], everywhere(L0_xattn_b_in),
                                  everywhere(L0_ffn_b)], axis=1),
        "ranks": np.concatenate([np.asarray(L0_ffn_V_r).T, np.asarray(L0_ffn_C).T], axis=1),
        "consts": con,
        "masks": msk,
    }
    nc = bacc.Bacc("TRN2", target_bir_lowering=False, num_devices=1)
    arrays, args = {}, []
    for name, a in laid.items():
        a = np.ascontiguousarray(a)
        arrays[f"in_{name}"] = a
        args.append(nc.dram_tensor(f"in_{name}", a.shape, mybir.dt.from_np(a.dtype), kind="ExternalInput").ap())
    out = nc.dram_tensor("out_x", (B, S, D), F32, kind="ExternalOutput").ap()
    build_gated_depool_ffn(nc, *args, out)
    r = run_bass_kernel_spmd(nc, [arrays], core_ids=[0])
    return r.results[0]["out_x"]
```

```python
from contextlib import ExitStack

import concourse.bass as bass
import numpy as np
from concourse import mybir

F32 = mybir.dt.float32
F32R = mybir.dt.float32r
F16 = mybir.dt.float16
BF16 = mybir.dt.bfloat16
I32 = mybir.dt.int32
ALU = mybir.AluOpType
ACT = mybir.ActivationFunctionType

B, S, D = 8, 512, 256
NP, DG = 1024, 512
R = 32
P = 128
KB = D // P
TPB = S // P
QT = S // P
EPS = 1e-5
LO = 16
HI = S // LO
PT = NP // P
EPS_DT = 0.001
DT = -np.log(-np.expm1(-EPS_DT))
C_DEC, C_CORN, C_LO, C_Q, C_END = 0, 128, 256, 272, 276
F_W, F_G, F_GATE, F_END = 0, KB * D, KB * D + KB, KB * D + KB + 2
S_W, S_GI, S_B1, S_B2, S_END = 0, KB * D, KB * D + D, KB * D + 2 * D, KB * D + 3 * D


def build_gated_depool_ffn(nc: bass.Bass, tiles, ctx, mask, first, second, ranks, consts, masks, out):
    es = ExitStack()
    with es:
        def sb(name, shape, dt=F32):
            return es.enter_context(nc.sbuf_tensor(name, shape, dt))

        def ps(name, shape):
            return es.enter_context(nc.psum_tensor(name, shape, F32))

        def sem(name):
            return es.enter_context(nc.semaphore(name))

        con = sb("con", [P, C_END])
        msk = sb("msk", [P, 2 * P + B], F16)
        decay_t = con[:, C_DEC:C_DEC + P]
        lo_eye = con[:, C_LO:C_LO + LO]
        q_index = con[:, C_Q:C_Q + 1]
        batch_prefix, batch_ones, batch_pick = msk[:, 0:P], msk[:, P:2 * P], msk[:, 2 * P:]
        ident = sb("ident", [P, P])
        neg_ident = sb("neg_ident", [P, P], F32R)
        first_sb = sb("first_sb", [P, F_END])
        second_sb = sb("second_sb", [P, S_END])
        ranks_sb = sb("ranks_sb", [R, 2 * D])
        mean_w = sb("mean_w", [P, P])
        tg = sb("tg", [P, 2])
        gates = first_sb[:, F_GATE:F_END]
        gres_sb = first_sb[:, F_G:F_GATE]
        w1_raw = first_sb[:, F_W:F_G].rearrange("p (k e) -> p k e", k=KB)
        w2_raw = second_sb[:, S_W:S_GI].rearrange("p (k e) -> p k e", k=KB)
        ginit_b = second_sb[:, S_GI:S_B1]
        b1_b = second_sb[:, S_B1:S_B2]
        b2_b = second_sb[:, S_B2:S_END]
        v_sb, c_sb = ranks_sb[:, 0:D], ranks_sb[:, D:2 * D]
        idle_w = sb("idle_w", [P, 2 * D], BF16)
        gain1 = sb("gain1", [P, KB])
        w1_g = sb("w1_g", [P, KB, D])
        w1_f = sb("w1_f", [P, KB, D])
        w1_hi = sb("w1_hi", [P, KB, D], F32R)
        w1_lo = sb("w1_lo", [P, KB, D], F32R)
        c_g = sb("c_g", [R, D])
        w2_s = sb("w2_s", [P, KB, D])
        w2_g = sb("w2_g", [P, KB, D])
        w2_f = sb("w2_f", [P, KB, D])
        w2_hi = sb("w2_hi", [P, KB, D], F32R)
        w2_lo = sb("w2_lo", [P, KB, D], F32R)
        lens = sb("lens", [B, NP], I32)
        one = sb("one", [P, 1])
        ends = sb("ends", [B, NP])
        wrap = sb("wrap", [P, PT * B])
        bidx = sb("bidx", [P, PT * B])
        bidx_i = sb("bidx_i", [P, PT * B], I32)
        bhi_i = sb("bhi_i", [P, PT * B], I32)
        blo_i = sb("blo_i", [P, PT * B], I32)
        bhi = sb("bhi", [P, PT * B], BF16)
        blo = sb("blo", [P, PT * B], BF16)
        iota_hi = sb("iota_hi", [P, HI, PT * B], BF16)
        hot_hi = sb("hot_hi", [P, HI, PT * B], BF16)
        hot_lo = sb("hot_lo", [P, LO, PT * B], BF16)
        bound = sb("bound", [HI, B * LO])
        bound_t = sb("bound_t", [P, HI], F16)
        row_scan = sb("row_scan", [P, HI])
        row_ex = sb("row_ex", [P, HI])
        count = sb("count", [P, HI])
        plug = sb("plug", [P, HI])
        plug_x = sb("plug_x", [P, S], F16)
        beyond = sb("beyond", [P, 1])
        flag = sb("flag", [1, 1], I32)
        in_sb = sb("in_sb", [P, 2, 2, 4 * D])
        x_sb = in_sb[:, :, :, 0:2 * D].rearrange("p q h (j d) -> p q h j d", j=2)
        xt_sb = in_sb[:, :, :, 2 * D:].rearrange("p q h (j k t) -> p q h j k t", j=2, k=KB)
        t_sb = sb("t_sb", [P, 2, 2, D])
        x1_sb = sb("x1_sb", [P, 2, 2, 2, D])
        out_sb = sb("out_sb", [P, 2, 2, 2, D])
        xt_hi = sb("xt_hi", [P, 2, 2, KB, P], F32R)
        xt_lo = sb("xt_lo", [P, 2, 2, KB, P], F32R)
        x1t_hi = sb("x1t_hi", [P, 2, 4, P], F32R)
        x1t_lo = sb("x1t_lo", [P, 2, 4, P], F32R)
        bn1 = sb("bn1", [P, 2, 2, 2, 6])
        mv1 = sb("mv1", [P, 2, 2, 2, 2])
        std1 = sb("std1", [P, 2, 2, 2])
        s1 = sb("s1", [P, 2, 2, 2])
        bn2 = sb("bn2", [P, 2, 2, 2, 6])
        mv2 = sb("mv2", [P, 2, 2, 2, 2])
        std2 = sb("std2", [P, 2, 2, 2])
        s2 = sb("s2", [P, 2, 2, 2])
        ctx_sb = sb("ctx_sb", [P, 2, DG])
        ctx_sq = sb("ctx_sq", [P, DG])
        c_ss = sb("c_ss", [P, 2])
        c_std = sb("c_std", [P, 2])
        c_r = sb("c_r", [P, 2])
        u_sb = sb("u_sb", [P, D])
        dp_f = sb("dp_f", [P, D])
        dp_hi = sb("dp_hi", [P, 2, D], F32R)
        dp_lo = sb("dp_lo", [P, 2, D], F32R)
        pick = sb("pick", [P, 2, TPB, P], F32R)

        g_ctx = sb("g_ctx", [P, QT, DG])
        g_ss = sb("g_ss", [P, QT])
        g_std = sb("g_std", [P, QT])
        g_inv = sb("g_inv", [P, QT])
        g_u = sb("g_u", [P, QT, D])
        g_dp = sb("g_dp", [P, QT, D])
        g_pick = sb("g_pick", [P, QT, S])
        r_x = sb("r_x", [P, TPB, D])
        g_n = sb("g_n", [P, TPB, D])
        g_t = sb("g_t", [P, TPB, KB, P])
        g_x1 = sb("g_x1", [P, TPB, D])
        g_bn = sb("g_bn", [P, TPB, 6])
        g_mv = sb("g_mv", [P, TPB, 2])

        g_ps = ps("g_ps", [P, 2, D])
        t2_ps = ps("t2_ps", [P, 4, P])
        a_ps = [ps(f"a_ps{n}", [P, 2, D]) for n in range(2)]
        b_ps = [ps(f"b_ps{n}", [P, 2, D]) for n in range(2)]
        dp_ps = ps("dp_ps", [P, 2 * D])
        plug_ps = ps("plug_ps", [P, S])
        ends_ps = g_ps[:].rearrange("p a b -> p (a b)")[:, 0:PT * B]
        count_ps = t2_ps[:].rearrange("p a b -> p (a b)")
        bound_ps = dp_ps[:, 0:HI]
        prefix_ps = plug_ps[:, 0:HI]
        total_ps = plug_ps[:, 256:256 + HI]
        corr_ps = b_ps[0]
        mean1_ps = a_ps[1][:, 0, :]
        mean2_ps = b_ps[1][:, 0, :]
        flag_ps = b_ps[0][0:1, 0, 0:1]

        out_v = out.rearrange("b (p h j) d -> b p h (j d)", p=P, h=2)

        names = ("lens_in", "gate_w_in", "con_in", "ranks_in", "second_in", "iotas", "consts_made", "ends_t", "scanned",
                 "idx", "hots", "counted", "bound_r", "bound_tr", "bound_h", "prefixed", "counts", "plugs",
                 "plug_xed", "flag_in", "flag_mm", "flag_set", "ident_made", "idle_made", "tanh_done", "gain1",
                 "w1_gained", "w1_mean", "w1_ready", "c_gated", "w2_scaled", "w2_corr", "w2_gated", "w2_mean", "w2_ready",
                 "w2_hi_ready", "w2_split", "b_scaled", "w1_hi_ready", "w1_split", "xt_hi_done", "xt_lo_done",
                 "a_done", "t_done", "tx_done", "g_done", "x1_done", "t2_done", "hi2", "lo2_mm", "lo2",
                 "b_done", "sums1", "stats1", "std1_s", "s1_done", "sums2", "stats2", "std2_s", "s2_done",
                 "x1b_done", "out_done", "ctx_sqd", "ctx_std", "ctx_r", "u_done", "dp_mm", "dpf_done",
                 "dph_done", "dpl_done", "plug_mm", "pick_done", "carrier")
        s = {n: sem(n) for n in names}
        x_in = [[sem(f"x_in{q}{h}") for h in range(2)] for q in range(2)]
        ctx_in = [sem(f"ctx_in{q}") for q in range(2)]
        out_free = [[sem(f"out_free{q}{h}") for h in range(2)] for q in range(2)]

        g = {n: sem("g_" + n) for n in (
            "stored", "ctx_in", "x_in", "squared", "ctx_std", "ctx_inv", "u", "scanned", "dp", "spread", "picks",
            "bn1", "mv1", "std1", "inv1", "xn", "t1", "t1_read", "mixed", "x1", "bn2", "mv2", "std2", "inv2",
            "t2", "t2_read", "product", "scaled", "out")}

        block = es.enter_context(nc.Block())

        def flagged(eng):
            eng.wait_ge(s["flag_set"], 1)
            return eng.value_load(flag[0:1, 0:1], min_val=0, max_val=P) > 0

        def wait(eng, name, value):
            if isinstance(value, int) and value <= 0:
                return
            eng.wait_ge(s[name], value)

        def wait_apart(eng, name, value):
            wait(eng, name, value)
            if not isinstance(value, int):
                eng.sem_inc(s["carrier"], 1)

        @block.sync
        def _(sp):
            sp.dma_start(lens[:], mask).then_inc(s["lens_in"], 16)

            def load_x(b, q, h):
                sp.dma_start(in_sb[:, q, h, :], tiles[b, h]).then_inc(x_in[q][h], 16)

            def load_ctx(b, q):
                sp.dma_start(ctx_sb[:, q, :], ctx[b, 0:P, :]).then_inc(ctx_in[q], 16)

            load_x(0, 0, 0)
            load_ctx(0, 0)
            sp.dma_start(ranks_sb[:], ranks).then_inc(s["ranks_in"], 16)
            sp.dma_start(second_sb[:], second).then_inc(s["second_in"], 16)
            load_x(0, 0, 1)
            load_x(1, 1, 0)
            load_ctx(1, 1)
            load_x(1, 1, 1)

            def step(b, q, load, store):
                i = 2 * b
                for h in (0, 1):
                    if load:
                        wait(sp, "tx_done", i + h + 1)
                        load_x(b + 2, q, h)
                        if h == 0:
                            wait(sp, "u_done", b + 1)
                            load_ctx(b + 2, q)
                    if store and isinstance(b, int) and b == B and h == 1:
                        for j in (0, 1):
                            wait(sp, "out_done", i + h - 1 + j)
                            sp.dma_start(out_v[b - 1, :, h, j * D:(j + 1) * D], out_sb[:, 1 - q, h, j, :]
                                         ).then_inc(out_free[1 - q][h], 16)
                    elif store:
                        wait(sp, "out_done", i + h - 1)
                        sp.dma_start(out_v[b - 1, :, h, :], out_sb[:, 1 - q, h, :, :].rearrange("p j d -> p (j d)")
                                     ).then_inc(out_free[1 - q][h], 16)

            step(0, 0, True, False)
            with sp.Fori(0, 2) as k:
                step(2 * k + 1, 1, True, True)
                step(2 * k + 2, 0, True, True)
            step(5, 1, True, True)
            for b in (6, 7, 8):
                step(b, b % 2, False, True)
            for q in (0, 1):
                for h in (0, 1):
                    sp.wait_ge(out_free[q][h], 16 * (B // 2 + 1 + q * h))
            with sp.If(flagged(sp)):
                sp.sem_inc(g["stored"], 16)
                with sp.Fori(0, B) as b:
                    sp.wait_ge(g["stored"], 16 * (b + 1))
                    sp.dma_start(g_ctx[:], ctx[bass.ds(b, 1), 0:S, :].rearrange("o (t p) d -> p (o t) d", p=P)
                                 ).then_inc(g["ctx_in"], 16)
                    sp.dma_start(r_x[:].rearrange("p (h j) d -> p h (j d)", h=2),
                                 tiles[bass.ds(b, 1), :, :, 0:2 * D].rearrange("o h p c -> p (o h) c")).then_inc(g["x_in"], 16)
                    sp.wait_ge(g["out"], b + 1)
                    sp.dma_start(out[bass.ds(b, 1)].rearrange("o (p j) d -> p (o j d)", p=P),
                                 g_n[:].rearrange("p j d -> p (j d)")).then_inc(g["stored"], 16)
                sp.wait_ge(g["stored"], 16 * (B + 1))
                sp.nop()
            sp.nop()

        @block.scalar
        def _(act):
            act.dma_start(first_sb[:], first).then_inc(s["gate_w_in"], 16)
            act.dma_start(con[:], consts).then_inc(s["con_in"], 16)
            act.dma_start(msk[:], masks).then_inc(s["con_in"], 16)
            act.wait_ge(s["gate_w_in"], 16)
            nc.scalar.activation(tg[:], gates, ACT.Tanh).then_inc(s["tanh_done"], 1)

            def ctx_squares(b, q):
                act.wait_ge(ctx_in[q], 16 * (b // 2 + 1) if isinstance(b, int) else 8 * (b - q) + 16)
                wait(act, "ctx_r", b - 1)
                nc.scalar.activation(ctx_sq[:], ctx_sb[:, q, :], ACT.Square,
                                     accum_out=c_ss[:, q:q + 1]).then_inc(s["ctx_sqd"], 1)

            def ctx_root(b, q):
                wait(act, "ctx_sqd", b + 1)
                nc.scalar.activation(c_std[:, q:q + 1], c_ss[:, q:q + 1], ACT.Sqrt, bias=con[:, C_Q + 1:C_Q + 2],
                                     scale=1.0 / DG).then_inc(s["ctx_std"], 1)

            def root1(i, q, h):
                wait(act, "stats1", i + 1)
                nc.scalar.activation(std1[:, q, h, :], mv1[:, q, h, :, 1], ACT.Sqrt, bias=con[:, C_Q + 2:C_Q + 3],
                                     scale=1.0 + EPS).then_inc(s["std1_s"], 1)

            def scale(i, q, h):
                wait(act, "a_done", i + 1)
                wait(act, "s1_done", i + 1)
                wait(act, "x1_done", i - 1)
                for j in (0, 1):
                    last = nc.scalar.activation(t_sb[:, h, j, :], a_ps[h][:, j, :], ACT.Copy, scale=s1[:, q, h, j:j + 1])
                last.then_inc(s["t_done"], 1)

            def root2(i, q, h):
                wait(act, "stats2", i + 1)
                nc.scalar.activation(std2[:, q, h, :], mv2[:, q, h, :, 1], ACT.Sqrt,
                                     bias=con[:, C_Q + 1:C_Q + 2]).then_inc(s["std2_s"], 1)

            def high1(i, q, h):
                act.wait_ge(x_in[q][h], 16 * (i // 4 + 1) if isinstance(i, int) else 4 * (i - (2 * q + h)) + 16)
                wait(act, "xt_lo_done", i - 4)
                nc.scalar.copy(xt_hi[:, h], xt_sb[:, q, h]).then_inc(s["xt_hi_done"], 1)

            def high2(i, h):
                wait(act, "t2_done", i + 1)
                nc.scalar.copy(x1t_hi[:, h], t2_ps[:]).then_inc(s["hi2"], 1)

            def low2(i, h):
                wait(act, "lo2_mm", i + 1)
                nc.scalar.copy(x1t_lo[:, h], t2_ps[:]).then_inc(s["lo2"], 1)

            def dp_high(b, q):
                wait(act, "dpf_done", b + 1)
                nc.scalar.copy(dp_hi[:, q, :], dp_f[:]).then_inc(s["dph_done"], 1)

            act.wait_ge(s["gain1"], 1)
            for k in range(KB):
                last = nc.scalar.activation(w1_g[:, k, :], w1_raw[:, k, :], ACT.Copy, scale=gain1[:, k:k + 1])
            last.then_inc(s["w1_gained"], 1)
            act.wait_ge(s["con_in"], 32)
            ctx_squares(0, 0)
            ctx_root(0, 0)
            act.wait_ge(s["ident_made"], 1)
            nc.scalar.mul(neg_ident[:], ident[:], -1.0)
            act.wait_ge(s["ranks_in"], 16)
            nc.scalar.mul(c_g[:], c_sb, tg[0:R, 1:2]).then_inc(s["c_gated"], 1)
            act.wait_ge(s["second_in"], 16)
            nc.scalar.mul(ginit_b, ginit_b, tg[:, 0:1]).then_inc(s["b_scaled"], 1)
            nc.scalar.mul(b1_b, b1_b, tg[:, 0:1]).then_inc(s["b_scaled"], 1)
            root1(0, 0, 0)
            nc.scalar.mul(w2_s[:], w2_raw, tg[:, 1:2]).then_inc(s["w2_scaled"], 1)
            nc.scalar.mul(b2_b, b2_b, tg[:, 1:2]).then_inc(s["b_scaled"], 1)
            act.wait_ge(s["w1_ready"], 1)
            nc.scalar.copy(w1_hi[:], w1_f[:]).then_inc(s["w1_hi_ready"], 1)
            dp_high(0, 0)
            root1(1, 0, 1)

            def second_weights():
                act.wait_ge(s["w2_ready"], 1)
                nc.scalar.copy(w2_hi[:], w2_f[:]).then_inc(s["w2_hi_ready"], 1)

            def step(b, q, first=False, last=False, over=False):
                i = 2 * b
                r = 1 - q
                for h in (0, 1):
                    nq, nh = (q, 1) if h == 0 else (r, 0)
                    pq, ph = (r, 1) if h == 0 else (q, 0)
                    has_next = not over and not (last and h == 1)
                    has_prev = not (first and h == 0) and not (over and h == 1)
                    ahead = not over and not last
                    if has_prev:
                        high2(i + h - 1, ph)
                        if first:
                            second_weights()
                        root2(i + h - 1, pq, ph)
                    if ahead and not (first and h == 0):
                        high1(i + h + 2, r, h)
                    if h == 0 and ahead:
                        ctx_squares(b + 1, r)
                        ctx_root(b + 1, r)
                    if has_prev:
                        low2(i + h - 1, ph)
                    if h == 1 and ahead:
                        dp_high(b + 1, r)
                    if has_next:
                        scale(i + h + 1, nq, nh)
                    if ahead:
                        root1(i + h + 2, r, h)

            step(0, 0, first=True)
            with act.Fori(0, 3) as k:
                step(2 * k + 1, 1)
                step(2 * k + 2, 0)
            step(7, 1, last=True)
            step(8, 0, over=True)

            with act.If(flagged(act)):
                with act.Fori(0, B) as b:
                    act.wait_ge(g["ctx_in"], 16 * (b + 1))
                    for t in range(QT):
                        last = nc.scalar.activation(ctx_sq[:], g_ctx[:, t, :], ACT.Square, accum_out=g_ss[:, t:t + 1])
                        last.then_inc(g["squared"], 1)
                        act.wait_ge(g["squared"], QT * b + t + 1)
                    nc.scalar.activation(g_std[:], g_ss[:], ACT.Sqrt, bias=con[:, C_Q + 1:C_Q + 2],
                                         scale=1.0 / DG).then_inc(g["ctx_std"], 1)
                    act.wait_ge(g["mv1"], b + 1)
                    act.wait_ge(g["ctx_inv"], b + 1)
                    nc.scalar.activation(g_std[:], g_mv[:, :, 1], ACT.Sqrt, bias=con[:, C_Q + 2:C_Q + 3],
                                         scale=1.0 + EPS).then_inc(g["std1"], 1)
                    act.wait_ge(g["mv2"], b + 1)
                    nc.scalar.activation(g_std[:], g_mv[:, :, 1], ACT.Sqrt,
                                         bias=con[:, C_Q + 1:C_Q + 2]).then_inc(g["std2"], 1)
                act.nop()
            act.nop()

        @block.vector
        def _(dve):
            V = nc.vector

            def sums(src, bn, sums_sem):
                V.bn_stats(bn[:, 0, :], src[:, 0, :])
                V.bn_stats(bn[:, 1, :], src[:, 1, :]).then_inc(s[sums_sem], 1)

            def mean_var(bn, mv, sums_sem, done, i):
                wait_apart(dve, sums_sem, i + 1)
                V.bn_aggr(mv[:, 0, :], bn[:, 0, :])
                V.bn_aggr(mv[:, 1, :], bn[:, 1, :]).then_inc(s[done], 1)

            def sums1(i, q, h):
                dve.wait_ge(x_in[q][h], 16 * (i // 4 + 1) if isinstance(i, int) else 4 * (i - (2 * q + h)) + 16)
                wait(dve, "t_done", i - 3)
                sums(x_sb[:, q, h], bn1[:, q, h], "sums1")

            def mean_var1(i, q, h):
                mean_var(bn1[:, q, h], mv1[:, q, h], "sums1", "stats1", i)

            def recip1(i, q, h):
                wait(dve, "std1_s", i + 1)
                V.reciprocal(s1[:, q, h, :], std1[:, q, h, :]).then_inc(s["s1_done"], 1)

            def recip2(i, q, h):
                wait(dve, "std2_s", i + 1)
                V.reciprocal(s2[:, q, h, :], std2[:, q, h, :]).then_inc(s["s2_done"], 1)

            def residual(i, q, h):
                wait(dve, "g_done", i + 1)
                wait(dve, "tx_done", i + 1)
                V.tensor_tensor(x1_sb[:, q, h], g_ps[:], t_sb[:, h], ALU.add).then_inc(s["x1_done"], 1)

            def sums2(i, q, h):
                wait(dve, "x1_done", i + 1)
                sums(x1_sb[:, q, h], bn2[:, q, h], "sums2")

            def mean_var2(i, q, h):
                mean_var(bn2[:, q, h], mv2[:, q, h], "sums2", "stats2", i)

            def finish(i, q, h, by_tile=False):
                wait(dve, "b_done", i + 1)
                wait(dve, "x1b_done", i + 1)
                wait(dve, "s2_done", i + 1)
                for j in (0, 1):
                    if by_tile and j == 1:
                        last.then_inc(s["out_done"], 1)
                        wait(dve, "b_done", i + 2)
                    bank = g_ps if by_tile and j == 1 else b_ps[h]
                    last = V.scalar_tensor_tensor(out=out_sb[:, q, h, j, :], in0=bank[:, j, :],
                                                  scalar=s2[:, q, h, j:j + 1], in1=out_sb[:, q, h, j, :],
                                                  op0=ALU.mult, op1=ALU.add)
                last.then_inc(s["out_done"], 1)

            def ctx_recip(b, q):
                wait(dve, "ctx_std", b + 1)
                V.reciprocal(c_r[:, q:q + 1], c_std[:, q:q + 1]).then_inc(s["ctx_r"], 1)

            def scale_ctx(b, q):
                wait(dve, "ctx_r", b + 1)
                wait(dve, "dp_mm", b)
                V.scalar_tensor_tensor(out=u_sb[:], in0=ctx_sb[:, q, 0:D], scalar=c_r[:, q:q + 1], in1=ginit_b,
                                       op0=ALU.mult, op1=ALU.mult).then_inc(s["u_done"], 1)

            def dp_bias(b):
                wait(dve, "dp_mm", b + 1)
                wait(dve, "dpl_done", b)
                V.tensor_tensor(dp_f[:], dp_ps[:, 0:D], b1_b, ALU.add).then_inc(s["dpf_done"], 1)

            def make_pick(b, q):
                wait(dve, "plug_mm", b + 1)
                wait(dve, "g_done", 2 * b - 2)
                V.tensor_scalar(pick[:, q].rearrange("p j t -> p (j t)"), plug_ps[:], q_index, None,
                                ALU.is_equal).then_inc(s["pick_done"], 1)

            V.memset(idle_w[:], 0.0).then_inc(s["idle_made"], 1)
            V.memset(one[:], 1.0).then_inc(s["scanned"], 1)
            dve.wait_ge(s["scanned"], 1)
            dve.wait_ge(s["lens_in"], 16)
            V.tensor_tensor_scan(ends[:], one[0:B, :].to_broadcast([B, NP]), lens[:], 0.0, ALU.mult, ALU.add
                                 ).then_inc(s["scanned"], 1)
            dve.wait_ge(s["ends_t"], 1)
            V.tensor_scalar(wrap[:], ends_ps, 0.5, float(S), ALU.is_lt, ALU.mult).then_inc(s["idx"], 1)
            dve.wait_ge(s["tanh_done"], 1)
            V.tensor_scalar(gain1[:], gres_sb, tg[:, 0:1], None, ALU.mult).then_inc(s["gain1"], 1)
            dve.wait_ge(s["idx"], 1)
            V.scalar_tensor_tensor(out=bidx[:], in0=ends_ps, scalar=-1.0, in1=wrap[:], op0=ALU.add,
                                   op1=ALU.add).then_inc(s["idx"], 1)
            dve.wait_ge(s["idx"], 2)
            V.tensor_scalar(bidx_i[:], bidx[:], -1.0, float(S), ALU.max, ALU.min).then_inc(s["idx"], 1)
            dve.wait_ge(s["idx"], 3)
            V.tensor_scalar(bhi_i[:], bidx_i[:], LO.bit_length() - 1, None, ALU.arith_shift_right)
            V.tensor_scalar(blo_i[:], bidx_i[:], LO - 1, None, ALU.bitwise_and).then_inc(s["idx"], 1)
            dve.wait_ge(s["idx"], 4)
            V.tensor_copy(bhi[:], bhi_i[:])
            V.tensor_copy(blo[:], blo_i[:]).then_inc(s["idx"], 1)
            dve.wait_ge(s["idx"], 5)
            dve.wait_ge(s["iotas"], 1)
            V.tensor_tensor(hot_hi[:], bhi[:].unsqueeze(1).to_broadcast([P, HI, PT * B]), iota_hi[:],
                            ALU.is_equal)
            V.tensor_tensor(hot_lo[:], blo[:].unsqueeze(1).to_broadcast([P, LO, PT * B]), iota_hi[:, 0:LO, :],
                            ALU.is_equal).then_inc(s["hots"], 1)
            ctx_recip(0, 0)
            dve.wait_ge(s["w1_mean"], 1)
            for k in range(KB):
                last = V.tensor_tensor(w1_f[:, k, :], w1_g[:, k, :], mean1_ps, ALU.subtract)
            last.then_inc(s["w1_ready"], 1)
            sums1(0, 0, 0)
            dve.wait_ge(s["counted"], 1)
            V.tensor_scalar(bound[:], count_ps[0:HI, 0:B * LO], 1.0, None, ALU.min).then_inc(s["bound_r"], 1)
            dve.wait_ge(s["b_scaled"], 1)
            scale_ctx(0, 0)
            dve.wait_ge(s["bound_tr"], 1)
            V.tensor_copy(bound_t[:], bound_ps).then_inc(s["bound_h"], 1)
            mean_var1(0, 0, 0)
            dve.wait_ge(s["prefixed"], 1)
            V.tensor_tensor_scan(row_scan[:], one[:].to_broadcast([P, HI]), total_ps, 0.0, ALU.mult, ALU.add
                                 ).then_inc(s["counts"], 1)
            dve.wait_ge(s["counts"], 1)
            V.tensor_tensor(row_ex[:], row_scan[:], total_ps, ALU.subtract).then_inc(s["counts"], 1)
            dve.wait_ge(s["counts"], 2)
            V.tensor_tensor(count[:], row_ex[:], prefix_ps, ALU.add).then_inc(s["counts"], 1)
            dve.wait_ge(s["counts"], 3)
            V.tensor_scalar(plug[:], count[:], -1.0, 0.0, ALU.add, ALU.max).then_inc(s["plugs"], 1)
            dve.wait_ge(s["plugs"], 1)
            V.tensor_tensor(plug_x[:].rearrange("p (j h a) -> p h a j", j=TPB, a=LO // TPB),
                            plug[:].unsqueeze(2).unsqueeze(3).to_broadcast([P, HI, LO // TPB, TPB]),
                            lo_eye.rearrange("p (a j) -> p a j", j=TPB).unsqueeze(1).to_broadcast([P, HI, LO // TPB, TPB]),
                            ALU.mult).then_inc(s["plug_xed"], 1)
            V.tensor_scalar(beyond[:], count[:, HI - 1:HI], float(P), None, ALU.is_gt).then_inc(s["flag_in"], 1)
            dve.wait_ge(s["b_scaled"], 2)
            dp_bias(0)
            recip1(0, 0, 0)
            make_pick(0, 0)
            dve.wait_ge(s["s1_done"], 1)
            dve.wait_ge(s["a_done"], 1)
            for j in (0, 1):
                last = V.scalar_tensor_tensor(out=t_sb[:, 0, j, :], in0=a_ps[0][:, j, :], scalar=s1[:, 0, 0, j:j + 1],
                                              in1=x_sb[:, 0, 0, j, :], op0=ALU.mult, op1=ALU.add)
            last.then_inc(s["tx_done"], 1)
            dve.wait_ge(s["tx_done"], 1)
            dve.sem_inc(s["t_done"], 1)
            sums1(1, 0, 1)
            mean_var1(1, 0, 1)

            def step(b, q, first=False, last=False, over=False):
                i = 2 * b
                r = 1 - q
                for h in (0, 1):
                    pq, ph = (r, 1) if h == 0 else (q, 0)
                    has_prev = not (first and h == 0) and not (over and h == 1)
                    ahead = not over and not last
                    if first and h == 0:
                        residual(0, 0, 0)
                        recip1(1, 0, 1)
                        dve.wait_ge(s["w2_scaled"], 1)
                        dve.wait_ge(s["w2_corr"], KB)
                        V.tensor_tensor(w2_g[:], w2_s[:], corr_ps[:], ALU.add).then_inc(s["w2_gated"], 1)
                    if first and h == 1:
                        dve.wait_ge(s["w2_mean"], 1)
                        for k in range(KB):
                            centred = V.tensor_tensor(w2_f[:, k, :], w2_g[:, k, :], mean2_ps, ALU.subtract)
                        centred.then_inc(s["w2_ready"], 1)
                    if ahead:
                        sums1(i + h + 2, r, h)
                    if h == 1 and ahead:
                        dp_bias(b + 1)
                    if first and h == 1:
                        dve.wait_ge(s["flag_mm"], 1)
                        V.tensor_copy(flag[:], flag_ps).then_inc(s["flag_set"], 1)
                    if not over and not (first and h == 0):
                        residual(i + h, q, h)
                    if h == 0 and ahead:
                        ctx_recip(b + 1, r)
                    if ahead:
                        mean_var1(i + h + 2, r, h)
                    if has_prev:
                        recip2(i + h - 1, pq, ph)
                    if h == 0 and ahead:
                        scale_ctx(b + 1, r)
                    if not over:
                        sums2(i + h, q, h)
                    if h == 1 and ahead:
                        make_pick(b + 1, r)
                    if not over:
                        mean_var2(i + h, q, h)
                    if ahead:
                        recip1(i + h + 2, r, h)
                    if not first:
                        finish(i + h - 2, r, h, by_tile=over and h == 1)

            step(0, 0, first=True)
            with dve.Fori(0, 3) as k:
                step(2 * k + 1, 1)
                step(2 * k + 2, 0)
            step(7, 1, last=True)
            step(8, 0, over=True)

            def stats_of(src, bn_sem, mv_sem, b):
                for j in range(TPB):
                    last = V.bn_stats(g_bn[:, j, :], src[:, j, :])
                last.then_inc(g[bn_sem], 1)
                dve.wait_ge(g[bn_sem], b + 1)
                dve.sem_inc(s["carrier"], 1)
                for j in range(TPB):
                    last = V.bn_aggr(g_mv[:, j, :], g_bn[:, j, :])
                last.then_inc(g[mv_sem], 1)

            def read_transposed(mm, read, b):
                dve.wait_ge(g[mm], b + 1)
                g_flat = g_ps[:].rearrange("p j d -> p (j d)")
                V.tensor_copy(g_t[:, 0:2].rearrange("p a b c -> p (a b c)"), g_flat)
                V.tensor_copy(g_t[:, 2:4].rearrange("p a b c -> p (a b) c"), t2_ps[:]).then_inc(g[read], 1)

            with dve.If(flagged(dve)):
                with dve.Fori(0, B) as b:
                    dve.wait_ge(g["ctx_std"], b + 1)
                    V.reciprocal(g_inv[:], g_std[:]).then_inc(g["ctx_inv"], 1)
                    dve.wait_ge(g["ctx_inv"], b + 1)
                    for t in range(QT):
                        last = V.scalar_tensor_tensor(out=g_u[:, t, :], in0=g_ctx[:, t, 0:D], scalar=g_inv[:, t:t + 1],
                                                      in1=ginit_b, op0=ALU.mult, op1=ALU.mult)
                    last.then_inc(g["u"], 1)
                    dve.wait_ge(g["x_in"], 16 * (b + 1))
                    stats_of(r_x, "bn1", "mv1", b)
                    dve.wait_ge(g["scanned"], b + 1)
                    for n in (0, 1):
                        last = V.tensor_tensor(g_dp[:, 2 * n:2 * n + 2, :], a_ps[n][:],
                                               b1_b.unsqueeze(1).to_broadcast([P, 2, D]), ALU.add)
                    last.then_inc(g["dp"], 1)
                    dve.wait_ge(g["spread"], b + 1)
                    for t in range(QT):
                        last = V.tensor_scalar(g_pick[:, t, :], plug_ps[:], float(-P * t), q_index, ALU.add, ALU.is_equal)
                    last.then_inc(g["picks"], 1)
                    dve.wait_ge(g["std1"], b + 1)
                    V.reciprocal(g_inv[:], g_std[:]).then_inc(g["inv1"], 1)
                    dve.wait_ge(g["inv1"], b + 1)
                    for j in range(TPB):
                        last = V.tensor_scalar(g_n[:, j, :], r_x[:, j, :], g_mv[:, j, 0:1], g_inv[:, j:j + 1],
                                               ALU.subtract, ALU.mult)
                    last.then_inc(g["xn"], 1)
                    read_transposed("t1", "t1_read", b)
                    dve.wait_ge(g["mixed"], b + 1)
                    for n in (0, 1):
                        last = V.tensor_tensor(g_x1[:, 2 * n:2 * n + 2, :], a_ps[n][:], r_x[:, 2 * n:2 * n + 2, :], ALU.add)
                    last.then_inc(g["x1"], 1)
                    dve.wait_ge(g["x1"], b + 1)
                    stats_of(g_x1, "bn2", "mv2", b)
                    read_transposed("t2", "t2_read", b)
                    dve.wait_ge(g["std2"], b + 1)
                    V.reciprocal(g_inv[:], g_std[:]).then_inc(g["inv2"], 1)
                    dve.wait_ge(g["inv2"], b + 1)
                    dve.wait_ge(g["product"], b + 1)
                    for j in range(TPB):
                        last = V.scalar_tensor_tensor(out=g_n[:, j, :], in0=b_ps[j // 2][:, j % 2, :],
                                                      scalar=g_inv[:, j:j + 1], in1=g_x1[:, j, :], op0=ALU.mult, op1=ALU.add)
                    last.then_inc(g["scaled"], 1)
                    dve.wait_ge(g["scaled"], b + 1)
                    V.tensor_tensor(g_n[:], g_n[:], b2_b.unsqueeze(1).to_broadcast([P, TPB, D]), ALU.add
                                    ).then_inc(g["out"], 1)
                dve.nop()
            dve.nop()

        @block.gpsimd
        def _(pool):
            G = nc.gpsimd
            G.memset(ident[:], 0.0).then_inc(s["consts_made"], 1)
            pool.wait_ge(s["consts_made"], 1)
            G.affine_select(out=ident[:], in_=ident[:], compare_op=ALU.not_equal, fill=1.0, base=0,
                            pattern=[[-1, P]], channel_multiplier=1).then_inc(s["ident_made"], 1)
            G.iota(iota_hi[:], [[1, HI], [0, PT * B]], base=0, channel_multiplier=0,
                   allow_small_or_imprecise_dtypes=True).then_inc(s["iotas"], 1)
            G.memset(mean_w[:], 1.0 / D).then_inc(s["consts_made"], 1)
            for q in (0, 1):
                for h in (0, 1):
                    pool.sem_inc(out_free[q][h], 16)

            def add_bias(i, q, h):
                wait(pool, "x1_done", i + 1)
                pool.wait_ge(out_free[q][h], 16 * (i // 4 + 1) if isinstance(i, int) else 4 * (i - (2 * q + h)) + 16)
                G.tensor_tensor(out_sb[:, q, h], x1_sb[:, q, h], b2_b.unsqueeze(1).to_broadcast([P, 2, D]),
                                ALU.add).then_inc(s["x1b_done"], 1)

            def low1(i, q, h):
                wait(pool, "xt_hi_done", i - 2)
                G.tensor_tensor(xt_lo[:, h], xt_sb[:, q, h], xt_hi[:, h].bitcast(F32),
                                ALU.subtract).then_inc(s["xt_lo_done"], 1)

            def add_x(i, q, h):
                wait(pool, "t_done", i + 1)
                G.tensor_tensor(t_sb[:, h], t_sb[:, h], x_sb[:, q, h], ALU.add).then_inc(s["tx_done"], 1)

            def dp_low(b, q):
                wait(pool, "dph_done", b + 1)
                G.tensor_tensor(dp_lo[:, q, :], dp_f[:], dp_hi[:, q, :].bitcast(F32), ALU.subtract).then_inc(s["dpl_done"], 1)

            dp_low(0, 0)
            pool.wait_ge(s["w1_hi_ready"], 1)
            G.tensor_tensor(w1_lo[:], w1_f[:], w1_hi[:].bitcast(F32), ALU.subtract).then_inc(s["w1_split"], 1)
            pool.wait_ge(s["b_scaled"], 3)

            def step(b, q, first=False, last=False, over=False):
                i = 2 * b
                r = 1 - q
                for h in (0, 1):
                    nq, nh = (q, 1) if h == 0 else (r, 0)
                    if first and h == 1:
                        pool.wait_ge(s["w2_hi_ready"], 1)
                        G.tensor_tensor(w2_lo[:], w2_f[:], w2_hi[:].bitcast(F32), ALU.subtract).then_inc(s["w2_split"], 1)
                    if not last and not (first and h == 0):
                        low1(i + h + 2, r, h)
                    if h == 1 and not last:
                        dp_low(b + 1, r)
                    if not (last and h == 1):
                        add_x(i + h + 1, nq, nh)
                    add_bias(i + h, q, h)

            step(0, 0, first=True)
            with pool.Fori(0, 3) as k:
                step(2 * k + 1, 1)
                step(2 * k + 2, 0)
            step(7, 1, last=True)

        @block.tensor
        def _(pe):
            T = nc.tensor

            def keep_warm(n, columns):
                for _ in range(n):
                    T.matmul(b_ps[1][:].rearrange("p j d -> p (j d)")[:, 0:columns], idle_w[:, 0:P],
                             idle_w[:, 0:columns], start=True, stop=True)

            def transpose2(i, q, h):
                wait(pe, "x1_done", i + 1)
                wait(pe, "lo2", i)
                for j in (0, 1):
                    for k in range(KB):
                        last = T.matmul(t2_ps[:, 2 * j + k, :], x1_sb[:, q, h, j, k * P:(k + 1) * P], ident[:],
                                        is_transpose=True, start=(j + k == 0), stop=True, skip_group_check=True)
                last.then_inc(s["t2_done"], 1)

            def low2(i, h):
                wait(pe, "hi2", i + 1)
                T.matmul(t2_ps[:].rearrange("p a b -> p (a b)"), neg_ident[:], x1t_hi[:, h].rearrange("p a b -> p (a b)"),
                         start=False, stop=True, skip_group_check=True).then_inc(s["lo2_mm"], 1)

            def product(bank, xh, xl, wh, wl):
                for k in range(KB):
                    for xs, ws in ((xh, wh), (xh, wl), (xl, wh)):
                        last = T.matmul(bank, xs[:, k, :], ws[:, k, :], start=k == 0 and ws is wh and xs is xh,
                                        stop=k == KB - 1 and xs is xl)
                return last

            def attend(i, q, h, tiles_of, split=False):
                if 0 in tiles_of:
                    pe.wait_ge(x_in[q][h], 16 * (i // 4 + 1) if isinstance(i, int) else 4 * (i - (2 * q + h)) + 16)
                    wait(pe, "t_done", i - 1)
                if split:
                    wait(pe, "xt_lo_done", i - 2)
                    for j in (0, 1):
                        last = product(a_ps[h][:, j, :], xt_hi[:, h, j], xt_lo[:, h, j], w1_hi, w1_lo)
                    last.then_inc(s["a_done"], 1)
                    return
                for j in tiles_of:
                    for k in range(KB):
                        last = T.matmul(a_ps[h][:, j, :], xt_sb[:, q, h, j, k, :], w1_f[:, k, :], start=k == 0,
                                        stop=k == KB - 1)
                if 1 in tiles_of:
                    last.then_inc(s["a_done"], 1)

            def gather(i, b, q, h):
                if h == 0:
                    wait(pe, "pick_done", b + 1)
                    wait(pe, "dpl_done", b + 1)
                wait(pe, "x1_done", i)
                for j in (0, 1):
                    for part in (dp_hi, dp_lo):
                        last = T.matmul(g_ps[:, j, :], pick[:, q, 2 * h + j, :], part[:, q, :], start=part is dp_hi,
                                        stop=part is dp_lo)
                last.then_inc(s["g_done"], 1)

            def ffn(i, h, by_tile=False):
                wait(pe, "lo2", i + 1)
                if isinstance(i, int):
                    wait(pe, "out_done", i - 1)
                for j in (0, 1):
                    bank = g_ps if by_tile and j == 1 else b_ps[h]
                    last = product(bank[:, j, :], x1t_hi[:, h, 2 * j:2 * j + 2], x1t_lo[:, h, 2 * j:2 * j + 2],
                                   w2_hi, w2_lo)
                    if by_tile and j == 0:
                        last.then_inc(s["b_done"], 1)
                last.then_inc(s["b_done"], 1)

            def scan(b):
                wait(pe, "u_done", b + 1)
                wait(pe, "dpf_done", b)
                T.matmul(dp_ps[:, 0:D], decay_t, u_sb[:], start=True, stop=True).then_inc(s["dp_mm"], 1)

            def spread(b):
                wait(pe, "plug_xed", 1)
                wait(pe, "pick_done", b)
                pick_b = batch_pick[:, b:b + 1] if isinstance(b, int) else batch_pick[:, bass.ds(b, 1)]
                T.matmul(plug_ps[:], pick_b.to_broadcast([P, P]), plug_x[:], start=True, stop=True).then_inc(s["plug_mm"], 1)

            def correct(k):
                pe.wait_ge(s["c_gated"], 1)
                T.matmul(corr_ps[:, k, :], v_sb[:, k * P:(k + 1) * P], c_g[:], start=True, stop=True
                         ).then_inc(s["w2_corr"], 1)

            pe.wait_ge(s["idle_made"], 1)
            keep_warm(7, 2 * D)
            pe.wait_ge(s["ident_made"], 1)
            pe.wait_ge(s["scanned"], 2)
            for j in range(PT):
                last = T.transpose(ends_ps[:, B * j:B * j + B], ends[:, j * P:(j + 1) * P], ident[0:B, 0:B])
            last.then_inc(s["ends_t"], 1)
            pe.wait_ge(s["consts_made"], 2)
            keep_warm(5, 2 * D)
            pe.wait_ge(s["w1_gained"], 1)
            for k in range(KB):
                last = T.matmul(mean1_ps, mean_w[:], w1_g[:, k, :], start=(k == 0), stop=(k == KB - 1))
            last.then_inc(s["w1_mean"], 1)
            pe.wait_ge(s["hots"], 1)
            for b in range(B):
                for j in range(PT):
                    last = T.matmul(count_ps[0:HI, b * LO:(b + 1) * LO], hot_hi[:, :, B * j + b], hot_lo[:, :, B * j + b],
                                    start=(j == 0), stop=(j == PT - 1))
            last.then_inc(s["counted"], 1)
            correct(0)
            pe.wait_ge(s["bound_r"], 1)
            T.transpose(bound_ps, bound[:], ident[0:HI, 0:HI]).then_inc(s["bound_tr"], 1)
            correct(1)
            pe.wait_ge(s["con_in"], 32)
            pe.wait_ge(s["bound_h"], 1)
            T.matmul(prefix_ps, batch_prefix, bound_t[:], start=True, stop=True)
            T.matmul(total_ps, batch_ones, bound_t[:], start=True, stop=True).then_inc(s["prefixed"], 1)
            scan(0)
            pe.wait_ge(s["w1_ready"], 1)
            attend(0, 0, 0, (0,))
            spread(0)
            attend(0, 0, 0, (1,))
            gather(0, 0, 0, 0)

            def step(b, q, first=False, last=False, over=False):
                i = 2 * b
                r = 1 - q
                for h in (0, 1):
                    nq, nh = (q, 1) if h == 0 else (r, 0)
                    pq, ph = (r, 1) if h == 0 else (q, 0)
                    has_next = not over and not (last and h == 1)
                    has_prev = not (first and h == 0) and not (over and h == 1)
                    if has_prev:
                        transpose2(i + h - 1, pq, ph)
                    if first and h == 1:
                        pe.wait_ge(s["w2_gated"], 1)
                        for k in range(KB):
                            summed = T.matmul(mean2_ps, mean_w[:], w2_g[:, k, :], start=(k == 0), stop=(k == KB - 1))
                        summed.then_inc(s["w2_mean"], 1)
                        pe.wait_ge(s["flag_in"], 1)
                        T.matmul(flag_ps, beyond[:], one[:], start=True, stop=True).then_inc(s["flag_mm"], 1)
                    if h == 1 and not over and not last:
                        spread(b + 1)
                        scan(b + 1)
                    if has_next:
                        attend(i + h + 1, nq, nh, (0, 1), split=not first)
                    if over and h == 0:
                        ffn(i - 2, h)
                    if has_prev:
                        low2(i + h - 1, ph)
                    if not over and not (first and h == 0):
                        gather(i + h, b, q, h)
                    if not first and not (over and h == 0):
                        ffn(i + h - 2, h, by_tile=over)

            step(0, 0, first=True)
            pe.wait_ge(s["w1_split"], 1)
            pe.wait_ge(s["w2_split"], 1)
            with pe.Fori(0, 3) as k:
                step(2 * k + 1, 1)
                step(2 * k + 2, 0)
            step(7, 1, last=True)
            step(8, 0, over=True)

            t1_ps = g_ps[:].rearrange("p j (k t) -> p (j k) t", k=KB)

            def transposed(src, j, bank):
                for k in range(KB):
                    last = T.transpose(bank[:, 2 * (j % 2) + k, :], src[:, j, k * P:(k + 1) * P], ident[:])
                return last

            with pe.If(flagged(pe)):
                with pe.Fori(0, B) as b:
                    pe.wait_ge(g["u"], b + 1)
                    for t in range(QT):
                        last = T.matmul(a_ps[t // 2][:, t % 2, :], decay_t, g_u[:, t, :], start=True, stop=t == 0)
                        if t:
                            last = T.matmul(a_ps[t // 2][:, t % 2, :], con[:, C_CORN:C_CORN + P], g_u[:, t - 1, :],
                                            start=False, stop=True)
                    last.then_inc(g["scanned"], 1)
                    T.matmul(plug_ps[:], batch_pick[:, bass.ds(b, 1)].to_broadcast([P, P]), plug_x[:], start=True,
                             stop=True).then_inc(g["spread"], 1)
                    pe.wait_ge(g["xn"], b + 1)
                    for j in range(TPB):
                        last = transposed(g_n, j, (t1_ps, t2_ps[:])[j // 2])
                    last.then_inc(g["t1"], 1)
                    pe.wait_ge(g["t1_read"], b + 1)
                    pe.wait_ge(g["picks"], b + 1)
                    pe.wait_ge(g["dp"], b + 1)
                    for j in range(TPB):
                        bank = a_ps[j // 2][:, j % 2, :]
                        for k in range(KB):
                            T.matmul(bank, g_t[:, j, k, :], w1_f[:, k, :], start=k == 0, stop=False)
                        for t in range(QT):
                            last = T.matmul(bank, g_pick[:, t, j * P:(j + 1) * P], g_dp[:, t, :], start=False, stop=t == QT - 1)
                    last.then_inc(g["mixed"], 1)
                    pe.wait_ge(g["x1"], b + 1)
                    for j in range(TPB):
                        last = transposed(g_x1, j, (t1_ps, t2_ps[:])[j // 2])
                    last.then_inc(g["t2"], 1)
                    pe.wait_ge(g["t2_read"], b + 1)
                    for j in range(TPB):
                        for k in range(KB):
                            last = T.matmul(b_ps[j // 2][:, j % 2, :], g_t[:, j, k, :], w2_f[:, k, :], start=k == 0,
                                            stop=k == KB - 1)
                    last.then_inc(g["product"], 1)
                pe.nop()
            pe.nop()


def shape_constants():
    n = np.arange(P)
    lag = n[None, :] - n[:, None]
    power = np.exp(-DT * np.maximum(lag, 0)) * np.exp(-EPS_DT)
    corner = np.exp(-DT * (lag + P)) * np.exp(-EPS_DT)
    con = np.zeros((P, C_END), np.float32)
    con[:, C_DEC:C_DEC + P] = np.where(lag >= 0, power, 0)
    con[:, C_CORN:C_CORN + P] = corner
    con[:, C_LO:C_LO + LO] = (n[:, None] % LO) == np.arange(LO)[None, :]
    con[:, C_Q] = n
    con[:, C_Q + 1] = EPS
    con[:, C_Q + 2] = EPS * EPS
    same = (n[:, None] // LO) == (n[None, :] // LO)
    msk = np.zeros((P, 2 * P + B), np.float16)
    msk[:, 0:P] = same & (n[:, None] <= n[None, :])
    msk[:, P:2 * P] = same
    msk[:, 2 * P:] = (n[:, None] // LO) == np.arange(B)[None, :]
    return con, msk


def kernel(x, ctx_2048, mask_BxS2_if0, g_xattn, g_ffn, L0_xattn_W_in, L0_xattn_b_in, L0_xattn_g_res,
           L0_xattn_g_init, L0_ffn_W, L0_ffn_b, L0_ffn_V_r, L0_ffn_C):
    import concourse.bacc as bacc
    from concourse.bass_utils import run_bass_kernel_spmd

    con, msk = shape_constants()
    def by_blocks(w):
        return np.asarray(w).T.reshape(KB, P, D).transpose(1, 0, 2).reshape(P, KB * D)

    def everywhere(v):
        v = np.asarray(v)
        return np.broadcast_to(v.reshape(1, v.size), (P, v.size))

    t = np.asarray(x).reshape(B, P, 2, 2, D)
    rows = t.transpose(0, 2, 1, 3, 4).reshape(B, 2, P, 2 * D)
    cols = t.reshape(B, P, 2, 2, KB, P).transpose(0, 2, 5, 3, 4, 1).reshape(B, 2, P, 2 * D)
    laid = {
        "x": np.concatenate([rows, cols], axis=3),
        "ctx": np.asarray(ctx_2048),
        "mask": np.asarray(mask_BxS2_if0),
        "first": np.concatenate([by_blocks(L0_xattn_W_in), np.asarray(L0_xattn_g_res).reshape(KB, P).T,
                                 everywhere(g_xattn), everywhere(g_ffn)], axis=1),
        "second": np.concatenate([by_blocks(L0_ffn_W), everywhere(L0_xattn_g_init)[:, 0:D], everywhere(L0_xattn_b_in),
                                  everywhere(L0_ffn_b)], axis=1),
        "ranks": np.concatenate([np.asarray(L0_ffn_V_r).T, np.asarray(L0_ffn_C).T], axis=1),
        "consts": con,
        "masks": msk,
    }
    nc = bacc.Bacc("TRN2", target_bir_lowering=False, num_devices=1)
    arrays, args = {}, []
    for name, a in laid.items():
        a = np.ascontiguousarray(a)
        arrays[f"in_{name}"] = a
        args.append(nc.dram_tensor(f"in_{name}", a.shape, mybir.dt.from_np(a.dtype), kind="ExternalInput").ap())
    out = nc.dram_tensor("out_x", (B, S, D), F32, kind="ExternalOutput").ap()
    build_gated_depool_ffn(nc, *args, out)
    r = run_bass_kernel_spmd(nc, [arrays], core_ids=[0])
    return r.results[0]["out_x"]
```
